# Optimizing a Trainium2 kernel written in Bass

```python
import numpy as np
import jax
import jax.numpy as jnp

def _softmax(x, axis=-1):
    return jax.nn.softmax(x, axis=axis)

def _gelu(x):
    return jax.nn.gelu(x, approximate=True)

def _silu(x):
    return jax.nn.silu(x)

def _sigmoid(x):
    return jax.nn.sigmoid(x)

def _layernorm(x, axis=-1, eps=1e-05):
    m = jnp.mean(x, axis=axis, keepdims=True)
    v = jnp.var(x, axis=axis, keepdims=True)
    return (x - m) / jnp.sqrt(v + eps)

def _scatter_add(tgt, idx, src, axis=0):
    return tgt.at[idx].add(src)

def _segment_sum(src, seg, n):
    return jax.ops.segment_sum(src, seg, n)
kernel_name = 'mk_gps_d1_gnn_r8_8db45e'

def setup_inputs(seed: int=0):
    np.random.seed(seed)
    _w = jnp.asarray

    def _rec_inputs():
        import jax
        import jax.numpy as jnp
        _gk = jax.random.key(seed)
        x = -8.776e-05 + 1 * jax.random.normal(jax.random.fold_in(_gk, 1), (6250, 512), jnp.float32)
        src = jax.random.randint(jax.random.fold_in(_gk, 2), (100000,), 0, 6250, jnp.int32)
        dst = jnp.minimum((6250 * jax.random.uniform(jax.random.fold_in(_gk, 3), (100000,)) ** 2.0).astype(jnp.int32), 49999)
        _o = jnp.argsort(dst, stable=True)
        src = src[_o]
        dst = dst[_o]
        return (x, src, dst)
    x, src, dst = _rec_inputs()

    def _L0_gnn_setup():
        import jax, jax.numpy as jnp
        import numpy as np
        N, E, D = (1250, 20000, 512)
        key = jax.random.key(seed)
        ks = jax.random.split(key, 5)
        x = jax.random.normal(ks[0], (N, D), dtype=jnp.float32)
        edge_index = jax.random.randint(ks[1], (2, E), 0, N, dtype=jnp.int32)
        W = jax.random.normal(ks[2], (D, D), dtype=jnp.float32) * (1.0 / np.sqrt(D))
        a_src = jax.random.normal(ks[3], (D,), dtype=jnp.float32) * 0.1
        a_dst = jax.random.normal(ks[4], (D,), dtype=jnp.float32) * 0.1
        bias = jnp.zeros((D,), dtype=jnp.float32)
        return {'x': x, 'edge_index': edge_index, 'W': W, 'a_src': a_src, 'a_dst': a_dst, 'bias': bias}
    _L0_gnn_all = _L0_gnn_setup()
    _L0_gnn_in = {k: v for k, v in _L0_gnn_all.items() if k in ('W', 'a_src', 'a_dst', 'bias')}
    del _L0_gnn_all

    def _L0_mix_setup():
        import jax, jax.numpy as jnp
        import numpy as np
        DIM = 512
        HEADS = 8

        def _reference_tuple_inner(x, Wqkv, temperature, Wproj, bproj):
            B, N, C = x.shape
            H = temperature.shape[0]
            D = C // H
            qkv = (x @ Wqkv.T).reshape(B, N, 3, H, D).transpose(2, 0, 3, 1, 4)
            q, k, v = (qkv[0], qkv[1], qkv[2])
            q = jax.nn.relu(q)
            k = jax.nn.relu(k)
            ksum = k.sum(axis=2)
            denom = jnp.clip(jnp.einsum('bhnd,bhd->bhn', q, ksum), 100.0)[..., None]
            attn = jnp.einsum('bhnd,bhne->bhde', k, v) * temperature
            attn1 = jnp.einsum('bhnd,bhde->bhne', q, attn)
            out = attn1 / denom
            y = out.transpose(0, 2, 1, 3).reshape(B, N, C) @ Wproj.T + bproj
            return (y, attn1)
        key = jax.random.key(seed)
        k1, k2, k3, k4 = jax.random.split(key, 4)
        head_dim = DIM // HEADS
        scale = head_dim ** (-0.5)
        x = jax.random.normal(k1, (4, 512, DIM), dtype=jnp.float32)
        Wqkv = jax.random.normal(k2, (3 * DIM, DIM), dtype=jnp.float32) * DIM ** (-0.5)
        temperature = jnp.ones((HEADS, 1, 1), dtype=jnp.float32) * scale
        Wproj = jax.random.normal(k3, (DIM, DIM), dtype=jnp.float32) * DIM ** (-0.5)
        bproj = jnp.zeros((DIM,), dtype=jnp.float32)
        return {'x': x, 'Wqkv': Wqkv, 'temperature': temperature, 'Wproj': Wproj, 'bproj': bproj}
    _L0_mix_all = _L0_mix_setup()
    _L0_mix_in = {k: v for k, v in _L0_mix_all.items() if k in ('Wqkv', 'temperature', 'Wproj', 'bproj')}
    del _L0_mix_all

    def _L0_ffn_setup():
        import jax, jax.numpy as jnp
        import numpy as np
        K = 2
        EPS = 1e-06

        def _layernorm(x, gamma, beta):
            mu = jnp.mean(x, axis=-1, keepdims=True)
            var = jnp.mean(jnp.square(x - mu), axis=-1, keepdims=True)
            return (x - mu) * jax.lax.rsqrt(var + EPS) * gamma + beta
        key = jax.random.key(seed)
        ks = jax.random.split(key, 5)
        B, S, D, F, E = (8, 256, 512, 256, 8)
        x = jax.random.normal(ks[0], (B, S, D), dtype=jnp.float32)
        router_w = jax.random.normal(ks[1], (D, E), dtype=jnp.float32) * 0.02
        w1 = jax.random.normal(ks[2], (E, D, F), dtype=jnp.float32) * 0.02
        b1 = jnp.zeros((E, F), dtype=jnp.float32)
        w2 = jax.random.normal(ks[3], (E, F, D), dtype=jnp.float32) * 0.02
        b2 = jnp.zeros((E, D), dtype=jnp.float32)
        gamma = jnp.ones((E, D), dtype=jnp.float32)
        beta = jnp.zeros((E, D), dtype=jnp.float32)
        return {'x': x, 'router_w': router_w, 'w1': w1, 'b1': b1, 'w2': w2, 'b2': b2, 'gamma': gamma, 'beta': beta}
    _L0_ffn_all = _L0_ffn_setup()
    _L0_ffn_in = {k: v for k, v in _L0_ffn_all.items() if k in ('router_w', 'w1', 'b1', 'w2', 'b2', 'gamma', 'beta')}
    del _L0_ffn_all
    return {'x': x, 'src': src, 'dst': dst, 'L0_gnn_W': _L0_gnn_in['W'], 'L0_gnn_a_src': _L0_gnn_in['a_src'], 'L0_gnn_a_dst': _L0_gnn_in['a_dst'], 'L0_gnn_bias': _L0_gnn_in['bias'], 'L0_mix_Wqkv': _L0_mix_in['Wqkv'], 'L0_mix_temperature': _L0_mix_in['temperature'], 'L0_mix_Wproj': _L0_mix_in['Wproj'], 'L0_mix_bproj': _L0_mix_in['bproj'], 'L0_ffn_router_w': _L0_ffn_in['router_w'], 'L0_ffn_w1': _L0_ffn_in['w1'], 'L0_ffn_b1': _L0_ffn_in['b1'], 'L0_ffn_w2': _L0_ffn_in['w2'], 'L0_ffn_b2': _L0_ffn_in['b2'], 'L0_ffn_gamma': _L0_ffn_in['gamma'], 'L0_ffn_beta': _L0_ffn_in['beta']}

def reference(x, src, dst, L0_gnn_W, L0_gnn_a_src, L0_gnn_a_dst, L0_gnn_bias, L0_mix_Wqkv, L0_mix_temperature, L0_mix_Wproj, L0_mix_bproj, L0_ffn_router_w, L0_ffn_w1, L0_ffn_b1, L0_ffn_w2, L0_ffn_b2, L0_ffn_gamma, L0_ffn_beta):
    import jax
    import jax.numpy as jnp

    def _L0_gnn_ref(x, edge_index, W, a_src, a_dst, bias):
        import jax, jax.numpy as jnp
        import numpy as np
        N, E, D = (1250, 20000, 512)
        n = x.shape[0]
        loops = jnp.arange(n, dtype=edge_index.dtype)
        src = jnp.concatenate([edge_index[0], loops])
        dst = jnp.concatenate([edge_index[1], loops])
        h = x @ W.T
        e_src = h @ a_src
        e_dst = h @ a_dst
        e = e_src[src] + e_dst[dst]
        neg_slope = 0.2
        e = jnp.where(e > 0, e, neg_slope * e)
        m = jax.ops.segment_max(e, dst, num_segments=n)
        e = jnp.exp(e - m[dst])
        s = jax.ops.segment_sum(e, dst, num_segments=n)
        alpha = e / s[dst]
        msg = alpha[:, None] * h[src]
        out = jax.ops.segment_sum(msg, dst, num_segments=n) + bias
        return x + jax.nn.elu(out)

    def _L0_mix_ref(x, Wqkv, temperature, Wproj, bproj):
        import jax, jax.numpy as jnp
        import numpy as np
        DIM = 512
        HEADS = 8

        def _reference_tuple_inner(x, Wqkv, temperature, Wproj, bproj):
            B, N, C = x.shape
            H = temperature.shape[0]
            D = C // H
            qkv = (x @ Wqkv.T).reshape(B, N, 3, H, D).transpose(2, 0, 3, 1, 4)
            q, k, v = (qkv[0], qkv[1], qkv[2])
            q = jax.nn.relu(q)
            k = jax.nn.relu(k)
            ksum = k.sum(axis=2)
            denom = jnp.clip(jnp.einsum('bhnd,bhd->bhn', q, ksum), 100.0)[..., None]
            attn = jnp.einsum('bhnd,bhne->bhde', k, v) * temperature
            attn1 = jnp.einsum('bhnd,bhde->bhne', q, attn)
            out = attn1 / denom
            y = out.transpose(0, 2, 1, 3).reshape(B, N, C) @ Wproj.T + bproj
            return (y, attn1)
        return _reference_tuple_inner(x, Wqkv, temperature, Wproj, bproj)[0]

    def _L0_ffn_ref(x, router_w, w1, b1, w2, b2, gamma, beta):
        import jax, jax.numpy as jnp
        import numpy as np
        K = 2
        EPS = 1e-06

        def _layernorm(x, gamma, beta):
            mu = jnp.mean(x, axis=-1, keepdims=True)
            var = jnp.mean(jnp.square(x - mu), axis=-1, keepdims=True)
            return (x - mu) * jax.lax.rsqrt(var + EPS) * gamma + beta
        B, S, D = x.shape
        E = w1.shape[0]
        xf = x.reshape(-1, D)
        logits = xf @ router_w
        gate_vals, idx = jax.lax.top_k(logits, K)
        gates = jax.nn.softmax(gate_vals, axis=-1)
        out = jnp.zeros_like(xf)
        for e in range(E):
            h = jax.nn.relu(xf @ w1[e] + b1[e]) @ w2[e] + b2[e]
            y = _layernorm(xf + h, gamma[e], beta[e])
            w = jnp.sum(jnp.where(idx == e, gates, 0.0), axis=-1)
            out = out + w[:, None] * y
        return out.reshape(B, S, D)
    edge_index = jnp.stack([src, dst])
    xn = _layernorm(x, axis=-1)
    x = x + _L0_gnn_ref(xn, edge_index, L0_gnn_W, L0_gnn_a_src, L0_gnn_a_dst, L0_gnn_bias) + _L0_mix_ref(xn[None], L0_mix_Wqkv, L0_mix_temperature, L0_mix_Wproj, L0_mix_bproj)[0]
    x = x + _L0_ffn_ref(_layernorm(x, axis=-1)[None], L0_ffn_router_w, L0_ffn_w1, L0_ffn_b1, L0_ffn_w2, L0_ffn_b2, L0_ffn_gamma, L0_ffn_beta)[0]
    return x

_drawn_inputs = setup_inputs


def setup_inputs(seed=0):
    import zlib

    import numpy as np

    out = dict(_drawn_inputs(seed))
    spreads = {'L0_gnn_bias': (0.0, 0.1),
     'L0_mix_temperature': (0.125, 0.6),
     'L0_mix_bproj': (0.0, 0.1),
     'L0_ffn_b1': (0.0, 0.8),
     'L0_ffn_b2': (0.0, 0.329),
     'L0_ffn_gamma': (1.0, 0.2),
     'L0_ffn_beta': (0.0, 0.343)}
    factors = {'L0_mix_Wqkv': 8.0, 'L0_mix_Wproj': 8.0, 'L0_ffn_w1': 2.754}
    for name, (base, spread) in spreads.items():
        noise = np.random.default_rng([zlib.crc32(name.encode()), seed]).standard_normal(out[name].shape)
        drawn = base * np.exp(spread * noise) if base else spread * noise
        out[name] = jnp.asarray(drawn.astype(out[name].dtype))
    for name, factor in factors.items():
        out[name] = (out[name] * factor).astype(out[name].dtype)
    return out
```

```python
from contextlib import ExitStack

import numpy as np

import concourse.bass as bass
from concourse import mybir

F32 = mybir.dt.float32
BF16 = mybir.dt.bfloat16
I32 = mybir.dt.int32
U32 = mybir.dt.uint32
ALU = mybir.AluOpType
ACT = mybir.ActivationFunctionType
AX = mybir.AxisListType
ds = bass.ds

P = 128
N, D, E = 6250, 512, 100000
NT = -(-N // P)
NP = NT * P
CH = 512
TPC = CH // P
VT = 8
HT = VT // 2
VE = VT * P
EP = 100 * VE
ET = EP // P
NC = EP // CH
assert EP >= E + VE
KC = D // P
NE, F = 8, 256
FC = F // P
ST = 2 * N // P + NE
assert ST <= P
LN_EPS, FFN_EPS = 1e-5, 1e-6
NO_NODE = 9999
ROWP = EP // VE
TB = ET // 8


def const_layout():
    parts = {
        "ident": np.eye(P),
        "iota_row": np.tile(np.arange(P), (P, 1)),
        "iota_col": np.arange(P)[:, None],
        "node_id": np.arange(NT)[None, :] * P + np.arange(P)[:, None],
        "tile_start": np.tile(np.arange(NT) * P, (P, 1)),
        "same_head": np.kron(np.eye(2), np.ones((64, 64))),
        "ones": np.ones((P, 1)),
        "ones_row": np.ones((P, P)),
        "minus_half": np.full((P, 1), -0.5),
        "ln_eps": np.full((P, 1), LN_EPS),
        "ffn_eps": np.full((P, 1), FFN_EPS),
        "tile_base": np.arange(P)[:, None] * P,
        "edge_tile_id": np.tile(np.arange(ET), (P, 1)),
        "before": np.triu(np.ones((P, P)), 1),
        "real": (np.arange(NT)[None, :] * P + np.arange(P)[:, None] < N) * 1.0,
        "past_end": (np.arange(NT)[None, :] * P + np.arange(P)[:, None] >= N) * float(P * P),
    }
    at, out = {}, 0
    for name, a in parts.items():
        at[name] = (out, out + a.shape[1])
        out += a.shape[1]
    return np.concatenate([parts[n] for n in parts], 1).astype(np.float32), at


def tiles(eng, n=NT):
    with eng.Fori(0, n // 2) as i:
        for s in (0, 1):
            yield 2 * i + s, s, i
    if n % 2:
        yield n - 1, 0, n // 2


class Steps:

    def __init__(self, eng, sem, k):
        self.eng, self.sem, self.k, self.base, self.n = eng, sem, k, 0, 0

    def round(self, r):
        assert self.n in (0, self.k), (self.n, self.k)
        self.base, self.n = r * self.k, 0

    def done(self, ins):
        self.n += 1
        ins.then_inc(self.sem, 1)

    def settle(self):
        self.eng.wait_ge(self.sem, self.base + self.n)


def gps_layer(nc, a, out):
    _, at = const_layout()
    dram = lambda name, shape, dt=F32: nc.dram_tensor(name, shape, dt).ap()
    h_rows = dram("h_rows", [NP, D])
    src_hi = dram("src_hi", [EP])
    es_rows = dram("es_rows", [EP])
    lo_hi = dram("lo_hi", [2, ET])
    ranges_d = dram("ranges_d", [NT, 4], I32)
    pq_rows = dram("pq_rows", [2, NP])
    x2_rows = dram("x2_rows", [NP, D])
    xf_rows = dram("xf_rows", [NP, D])
    y_rows = dram("y_rows", [ST * P, D])

    with ExitStack() as whole:
        def sem(name):
            return whole.enter_context(nc.semaphore(name))

        def sb(scope, name, shape, dt=F32):
            return scope.enter_context(nc.sbuf_tensor(name, shape, dt))

        def psum(scope, name, shape=(P, D), dt=F32):
            return scope.enter_context(nc.psum_tensor(name, list(shape), dt))

        held = {}

        def hold(eng, s, value):
            name = str(eng.engine)
            if name not in held:
                held[name] = sem(f"held_{len(held)}")
            eng.wait_ge(s, value)
            eng.sem_inc(held[name], 1)

        cst = sb(whole, "cst", list(a["consts"].shape))
        C = {n: cst[:, lo:hi] for n, (lo, hi) in at.items()}

        graph = whole.enter_context(ExitStack())
        qT = sb(graph, "qT", [P, KC, NP])
        src_col = sb(graph, "src_col", [P, ET], I32)
        dst_col = sb(graph, "dst_col", [P, ET])
        lo_col = sb(graph, "lo_col", [P, ET])
        es_col = sb(graph, "es_col", [P, ET])
        es2_col = sb(graph, "es2_col", [P, ET])
        esed = sb(graph, "esed", [P, NT, 2])
        ln_keep = sb(graph, "ln_keep", [P, NT, 2])
        kb_head = sb(graph, "kb_head", [P, KC, P])
        fold_w = sb(graph, "fold_w", [P, KC, D])
        es_lut = sb(graph, "es_lut", [NT, P])
        ranges = sb(graph, "ranges", [1, NT * 4], I32)
        es_floor = sb(graph, "es_floor", [P, 2])
        peak = sb(graph, "peak", [P, NT])
        w_self = sb(graph, "w_self", [P, NT])

        with ExitStack() as sc:
            wg = sb(sc, "wg", [P, KC, D])
            wqkv = sb(sc, "wqkv", [P, KC, 3 * D])
            wproj = sb(sc, "wproj", [P, KC, D])
            temp = sb(sc, "temp", [P, KC])
            u = sb(sc, "u", [P, KC, 2])
            ps = ExitStack()
            w_nat = sb(ps, "w_nat", [P, KC, D])
            avec = sb(ps, "avec", [P, KC, 2])
            dst_i = sb(ps, "dst_i", [P, ET], I32)
            lin_i = sb(ps, "lin_i", [ROWP, EP // ROWP], I32)
            lin_f = sb(ps, "lin_f", [ROWP, EP // ROWP])
            lohi_sb = sb(ps, "lohi_sb", [ROWP, 2, VT])
            lohi_bc = sb(ps, "lohi_bc", [NT, 2, ET])
            rtmp = sb(ps, "rtmp", [NT, ET])
            rout = sb(ps, "rout", [NT, 4])
            rout_i = sb(ps, "rout_i", [NT, 4], I32)
            loaded = sem("setup_loaded")
            ints = sem("setup_ints")
            saved = sem("setup_saved")
            r_loaded = sem("range_loaded")
            tri = sem("range_offsets")
            with ps:
                u_ps = psum(ps, "u_ps")
                off_ps = psum(ps, "off_ps")
                u_done = sem("u_done")
                with nc.Block() as block:
                    @block.sync
                    def _(sp):
                        for dst, src in ((cst[:], a["consts"]), (wg[:], a["wg"]), (w_nat[:], a["w_nat"]),
                                         (wqkv[:], a["wqkv"]), (wproj[:], a["wproj"]), (avec[:], a["avec"]),
                                         (temp[:], a["temp"]), (src_col[:], a["src_col"]),
                                         (dst_i[:], a["dst_col"]), (lin_i[:], a["dst_lin"])):
                            sp.dma_start(dst, src).then_inc(loaded, 16)
                        sp.wait_ge(ints, 3)
                        for k in range(2):
                            sp.dma_start(lo_hi[k].rearrange("(p c) -> p c", c=VT), lohi_sb[:, k, :]).then_inc(saved, 16)
                        sp.dma_start(lin_i[:], a["src_lin"]).then_inc(loaded, 16)
                        sp.wait_ge(saved, 32)
                        sp.dma_start(lohi_bc[:], lo_hi.partition_broadcast(NT)).then_inc(r_loaded, 16)
                        sp.wait_ge(ints, 5)
                        sp.dma_start(src_hi.rearrange("(p c) -> p c", p=ROWP), lin_f[:]).then_inc(saved, 16)
                        sp.wait_ge(ints, 23)
                        sp.dma_start(ranges_d, rout_i[:]).then_inc(saved, 16)
                        sp.wait_ge(saved, 64)
                        sp.dma_start(ranges[:], ranges_d.rearrange("(o t) c -> o (t c)", o=1)).then_inc(r_loaded, 16)
                        sp.wait_ge(r_loaded, 32)

                    @block.tensor
                    def _(pe):
                        pe.wait_ge(loaded, 160)
                        for k in range(KC):
                            for j in range(KC):
                                last = nc.tensor.matmul(u_ps[:, 2 * k:2 * k + 2], w_nat[:, j, k * P:(k + 1) * P],
                                                        avec[:, j, :], start=(j == 0), stop=(j == KC - 1))
                        last.then_inc(u_done, 1)
                        pe.wait_ge(ints, 19)
                        nc.tensor.matmul(off_ps[0:NT, 0:1], C["before"][0:NT, 0:NT], rout[:, 1:2],
                                         start=True, stop=True).then_inc(tri, 1)

                    @block.vector
                    def _(dve):
                        step = Steps(dve, ints, 0)
                        dve.wait_ge(loaded, 160)
                        lin3 = lin_i[:].rearrange("p (c e) -> p c e", c=VT)
                        step.done(nc.vector.tensor_reduce(lohi_sb[:, 0, :], lin3, AX.X, ALU.min))
                        step.done(nc.vector.tensor_reduce(lohi_sb[:, 1, :], lin3, AX.X, ALU.max))
                        step.done(nc.vector.tensor_copy(dst_col[:], dst_i[:]))
                        dve.wait_ge(loaded, 176)
                        step.settle()
                        step.done(nc.vector.tensor_scalar(lin_i[:], lin_i[:], 7, None, ALU.arith_shift_right))
                        step.settle()
                        step.done(nc.vector.tensor_copy(lin_f[:], lin_i[:]))
                        step.done(nc.vector.tensor_scalar(dst_i[:], src_col[:], 127, None, ALU.bitwise_and))
                        step.settle()
                        step.done(nc.vector.tensor_copy(lo_col[:], dst_i[:]))
                        dve.wait_ge(r_loaded, 16)
                        base = C["tile_base"][0:NT, :]
                        cid = C["edge_tile_id"][0:NT, :]
                        step.done(nc.vector.tensor_scalar(rtmp[:], lohi_bc[:, 0, :], base, float(P - 1),
                                                          ALU.subtract, ALU.is_le))
                        step.settle()
                        step.done(nc.vector.scalar_tensor_tensor(rtmp[:], lohi_bc[:, 1, :], base, rtmp[:],
                                                                 ALU.is_ge, ALU.mult))
                        step.settle()
                        step.done(nc.vector.scalar_tensor_tensor(lohi_bc[:, 0, :], rtmp[:], -1000.0, cid,
                                                                 ALU.mult, ALU.add))
                        step.done(nc.vector.scalar_tensor_tensor(lohi_bc[:, 1, :], cid, 1.0, rtmp[:],
                                                                 ALU.add, ALU.mult))
                        step.settle()
                        step.done(nc.vector.tensor_reduce(rout[:, 0:1], lohi_bc[:, 0, :], AX.X, ALU.min))
                        step.done(nc.vector.tensor_reduce(rout[:, 1:2], lohi_bc[:, 1, :], AX.X, ALU.max))
                        step.settle()
                        step.done(nc.vector.tensor_scalar(rout[:, 0:1], rout[:, 0:1], 1000.0, float(ET - VT),
                                                          ALU.add, ALU.min))
                        step.settle()
                        step.done(nc.vector.scalar_tensor_tensor(rout[:, 1:2], rout[:, 1:2], float(VT - 1), rout[:, 0:1],
                                                                 ALU.add, ALU.subtract))
                        step.settle()
                        step.done(nc.vector.tensor_copy(rout_i[:, 1:2], rout[:, 1:2]))
                        step.settle()
                        step.done(nc.vector.tensor_scalar(rout_i[:, 3:4], rout_i[:, 1:2], VT.bit_length() - 1, None, ALU.arith_shift_right))
                        step.settle()
                        step.done(nc.vector.tensor_copy(rout[:, 2:3], rout_i[:, 3:4]))
                        step.settle()
                        step.done(nc.vector.tensor_scalar(rout[:, 1:2], rout[:, 2:3], 1.0, None, ALU.max))
                        assert step.n == 19
                        dve.wait_ge(tri, 1)
                        step.settle()
                        step.done(nc.vector.scalar_tensor_tensor(rout[:, 2:3], off_ps[0:NT, 0:1], float(VT), rout[:, 0:1],
                                                                 ALU.mult, ALU.subtract))
                        step.done(nc.vector.scalar_tensor_tensor(rout[:, 3:4], rout[:, 1:2], float(VT), rout[:, 0:1],
                                                                 ALU.mult, ALU.add))
                        step.settle()
                        step.done(nc.vector.tensor_scalar(rout[:, 1:2], rout[:, 3:4], float(1 - VT), None, ALU.add))
                        step.settle()
                        step.done(nc.vector.tensor_copy(rout_i[:], rout[:]))
                        dve.wait_ge(u_done, 1)
                        nc.vector.tensor_copy(u[:].rearrange("p c o -> p (c o)"), u_ps[:, 0:2 * KC]).then_inc(ints, 1)

            with ExitStack() as pj:
                xb = [sb(pj, f"xb{s}", [P, D]) for s in (0, 1)]
                xn = [sb(pj, f"xn{s}", [P, D]) for s in (0, 1)]
                xnT = [sb(pj, f"xnT{s}", [P, KC, P]) for s in (0, 1)]
                hb = [sb(pj, f"hb{s}", [P, D]) for s in (0, 1)]
                kb = [sb(pj, f"kb{s}", [P, D]) for s in (0, 1)]
                vb = [sb(pj, f"vb{s}", [P, D]) for s in (0, 1)]
                bn = [sb(pj, f"bn{s}", [P, 6]) for s in (0, 1)]
                mv = [sb(pj, f"mv{s}", [P, 2]) for s in (0, 1)]
                sd = [sb(pj, f"sd{s}", [P, 2]) for s in (0, 1)]
                zero = sb(pj, "zero", [P, D])
                T_ps, h_ps, k_ps, v_ps, q_ps = (psum(pj, n) for n in ("T_ps", "h_ps", "k_ps", "v_ps", "q_ps"))
                kv_ps, ks_ps, e_ps = (psum(pj, n) for n in ("kv_ps", "ks_ps", "e_ps"))
                x_in = [sem(f"x_in{s}") for s in (0, 1)]
                h_out = [sem(f"h_out{s}") for s in (0, 1)]
                x_free, xn_ready, rstd_ready, mv_ready = sem("x_free"), sem("xn_ready"), sem("rstd_ready"), sem("mv_ready")
                T_ready, xnT_ready, h_done, k_done, v_done, q_done = (sem(n) for n in (
                    "T_ready", "xnT_ready", "h_done", "k_done", "v_done", "q_done"))
                hb_ready, kb_ready, vb_ready, h_free, q_free = (sem(n) for n in (
                    "hb_ready", "kb_ready", "vb_ready", "h_free", "q_free"))
                bn_ready, var_ready, kv_done, zeroed = sem("bn_ready"), sem("var_ready"), sem("kv_done"), sem("zeroed")

                with nc.Block() as block:
                    @block.sync
                    def _(sp):
                        sp.sem_inc(x_free, 2)
                        for t, s, i in tiles(sp):
                            sp.wait_ge(x_free, t + 1)
                            sp.dma_start(xb[s][:], a["x"][ds(t * P, P), :]).then_inc(x_in[s], 16)

                    @block.gpsimd
                    def _(pool):
                        nc.gpsimd.memset(zero[:], 0.0).then_inc(zeroed, 1)
                        for t, s, i in tiles(pool):
                            pool.wait_ge(mv_ready, t + 1)
                            nc.gpsimd.tensor_tensor(sd[s][:, 0:1], mv[s][:, 1:2], C["ln_eps"], ALU.add).then_inc(var_ready, 1)
                            pool.wait_ge(var_ready, t + 1)
                            nc.gpsimd.tensor_tensor(sd[s][:, 1:2], sd[s][:, 0:1], C["minus_half"], ALU.pow).then_inc(rstd_ready, 1)

                    @block.vector
                    def _(dve):
                        dve.sem_inc(h_free, 1)

                        def norm(t, s, i):
                            dve.wait_ge(x_in[s], 16 * i + 16)
                            nc.vector.bn_stats(bn[s][:], xb[s][:]).then_inc(bn_ready, 1)
                            hold(dve, bn_ready, t + 1)
                            nc.vector.bn_aggr(mv[s][:], bn[s][:]).then_inc(mv_ready, 1)
                            dve.wait_ge(rstd_ready, t + 1)
                            dve.wait_ge(mv_ready, t + 1)
                            nc.vector.tensor_scalar(xn[s][:], xb[s][:], mv[s][:, 0:1], sd[s][:, 1:2],
                                                    ALU.subtract, ALU.mult).then_inc(xn_ready, 1)
                            nc.vector.tensor_scalar(ln_keep[:, ds(t, 1), 0], sd[s][:, 1:2], 1.0, None, ALU.add)
                            nc.vector.scalar_tensor_tensor(ln_keep[:, ds(t, 1), 1], mv[s][:, 0:1], -1.0, sd[s][:, 1:2],
                                                           ALU.mult, ALU.mult).then_inc(x_free, 1)

                        norm(0, 0, 0)
                        for t, s, i in tiles(dve):
                            dve.wait_ge(h_done, t + 1)
                            if not isinstance(t, int):
                                norm(t + 1, 1 - s, i + s)
                            dve.wait_ge(h_out[s], 16 * i + 16)
                            nc.vector.tensor_copy(hb[s][:], h_ps[:]).then_inc(hb_ready, 1)
                            nc.vector.tensor_copy(esed[:, ds(t, 1), :], e_ps[:, 0:2].unsqueeze(1)).then_inc(h_free, 1)
                            dve.wait_ge(v_done, t + 1)
                            nc.vector.tensor_copy(vb[s][:], v_ps[:]).then_inc(vb_ready, 1)

                    @block.scalar
                    def _(act):
                        act.sem_inc(q_free, 1)
                        for s in (0, 1):
                            act.sem_inc(h_out[s], 16)
                        for t, s, i in tiles(act):
                            act.wait_ge(T_ready, t + 1)
                            nc.scalar.copy(xnT[s][:].rearrange("p c k -> p (c k)"), T_ps[:]).then_inc(xnT_ready, 1)
                            act.wait_ge(k_done, t + 1)
                            nc.scalar.activation(kb[s][:], k_ps[:], ACT.Relu).then_inc(kb_ready, 1)
                            act.wait_ge(hb_ready, t + 1)
                            act.dma_start(h_rows[ds(t * P, P), :], hb[s][:]).then_inc(h_out[s], 16)
                            hold(act, q_done, t + 1)
                            nc.scalar.activation(qT[:, :, ds(t * P, P)], q_ps[:].rearrange("p (c k) -> p c k", c=KC),
                                                 ACT.Relu).then_inc(q_free, 1)
                        act.wait_ge(h_out[0], 16 * (NT // 2 + 2))
                        act.wait_ge(h_out[1], 16 * (NT // 2 + 1))

                    @block.tensor
                    def _(pe):
                        def transposes(t, s):
                            pe.wait_ge(xn_ready, t + 1)
                            for c in range(KC):
                                last = nc.tensor.transpose(T_ps[:, c * P:(c + 1) * P], xn[s][:, c * P:(c + 1) * P], C["ident"])
                            last.then_inc(T_ready, 1)

                        pe.wait_ge(zeroed, 1)
                        nc.tensor.matmul(kv_ps[:], zero[:, 0:P], zero[:], start=True, stop=False, skip_group_check=True)
                        nc.tensor.matmul(ks_ps[:, 0:KC], zero[:, 0:P], zero[:, 0:KC], start=True, stop=False, skip_group_check=True)
                        transposes(0, 0)
                        for t, s, i in tiles(pe):
                            pe.wait_ge(xnT_ready, t + 1)
                            pe.wait_ge(h_free, t + 1)
                            for c in range(KC):
                                nc.tensor.matmul(h_ps[:], xnT[s][:, c, :], wg[:, c, :], start=(c == 0), stop=(c == KC - 1))
                            for c in range(KC):
                                last = nc.tensor.matmul(e_ps[:, 0:2], xnT[s][:, c, :], u[:, c, :], start=(c == 0), stop=(c == KC - 1))
                            last.then_inc(h_done, 1)
                            for c in range(KC):
                                last = nc.tensor.matmul(k_ps[:], xnT[s][:, c, :], wqkv[:, c, D:2 * D], start=(c == 0), stop=(c == KC - 1))
                            last.then_inc(k_done, 1)
                            if not isinstance(t, int):
                                transposes(t + 1, 1 - s)
                            for c in range(KC):
                                last = nc.tensor.matmul(v_ps[:], xnT[s][:, c, :], wqkv[:, c, 2 * D:3 * D], start=(c == 0), stop=(c == KC - 1))
                            last.then_inc(v_done, 1)
                            pe.wait_ge(q_free, t + 1)
                            for j in range(KC):
                                for c in range(KC):
                                    last = nc.tensor.matmul(q_ps[:, j * P:(j + 1) * P], wqkv[:, c, j * P:(j + 1) * P], xnT[s][:, c, :],
                                                            start=(c == 0), stop=(c == KC - 1))
                            last.then_inc(q_done, 1)
                            pe.wait_ge(kb_ready, t + 1)
                            pe.wait_ge(vb_ready, t + 1)
                            for c in range(KC):
                                cs = slice(c * P, (c + 1) * P)
                                nc.tensor.matmul(kv_ps[:, cs], vb[s][:, cs], kb[s][:, cs], start=False, stop=False, skip_group_check=True)
                                nc.tensor.matmul(ks_ps[:, c:c + 1], kb[s][:, cs], C["ones"], start=False, stop=False, skip_group_check=True)
                        nc.tensor.matmul(kv_ps[:], zero[:, 0:P], zero[:], start=False, stop=True, skip_group_check=True)
                        nc.tensor.matmul(ks_ps[:, 0:KC], zero[:, 0:P], zero[:, 0:KC], start=False, stop=True, skip_group_check=True).then_inc(kv_done, 1)

                with ExitStack() as fo:
                    abT = sb(fo, "abT", [P, KC, P])
                    ks_sb = sb(fo, "ks_sb", [P, KC])
                    lut_d = sb(fo, "lut_d", [NT, P])
                    lows = sb(fo, "lows", [P, 2])
                    fold_dve, fold_pe, fold_pool = sem("fold_dve"), sem("fold_pe"), sem("fold_pool")
                    with nc.Block() as block:
                        @block.vector
                        def _(dve):
                            for c in range(KC):
                                nc.vector.scalar_tensor_tensor(abT[:, c, :], kv_ps[:, c * P:(c + 1) * P], temp[:, c:c + 1],
                                                               C["same_head"], ALU.mult, ALU.mult).then_inc(fold_dve, 1)
                            nc.vector.tensor_copy(ks_sb[:], ks_ps[:, 0:KC]).then_inc(fold_dve, 1)
                            dve.wait_ge(fold_dve, 5)
                            for c in range(KC):
                                nc.vector.tensor_scalar(kb_head[:, c, :], C["same_head"], ks_sb[:, c:c + 1], None, ALU.mult)
                            for c in range(KC):
                                dve.wait_ge(fold_pe, c + 1)
                                nc.vector.tensor_copy(fold_w[:, c, :], (h_ps, k_ps, v_ps, q_ps)[c][:])
                            dve.wait_ge(fold_pe, KC + 1)
                            nc.vector.tensor_copy(es_lut[:], T_ps[0:NT, 0:P])
                            nc.vector.tensor_reduce(lows[:, 0:1], esed[:, :, 0], AX.X, ALU.min).then_inc(fold_dve, 1)
                            dve.wait_ge(fold_dve, 6)
                            nc.vector.tensor_scalar(lows[:, 1:2], lows[:, 0:1], -1.0, None, ALU.mult).then_inc(fold_dve, 1)
                            dve.wait_ge(fold_pool, 1)
                            nc.vector.tensor_scalar(es_floor[:, 0:1], lows[:, 0:1], -1.0, None, ALU.mult)
                            nc.vector.tensor_copy(es_floor[:, 1:2], lows[:, 0:1])

                        @block.gpsimd
                        def _(pool):
                            pool.wait_ge(fold_dve, 7)
                            nc.gpsimd.partition_all_reduce(lows[:, 0:1], lows[:, 1:2], P, bass.bass_isa.ReduceOp.max).then_inc(fold_pool, 1)

                        @block.tensor
                        def _(pe):
                            for c in range(KC):
                                pe.wait_ge(fold_dve, c + 1)
                                nc.tensor.matmul((h_ps, k_ps, v_ps, q_ps)[c][:], abT[:, c, :], wproj[:, c, :],
                                                 start=True, stop=True).then_inc(fold_pe, 1)
                            nc.tensor.transpose(T_ps[0:NT, 0:P], esed[:, :, 0], C["ident"]).then_inc(fold_pe, 1)

        R = 4
        with ExitStack() as lk:
            hi_row = [sb(lk, f"hi_row{s}", [NT, CH]) for s in range(R)]
            hot = [sb(lk, f"hot{s}", [NT, CH]) for s in range(R)]
            picked = sb(lk, "picked", [P, R * TPC, P])
            er = sb(lk, "er", [TB, 8, P])
            row_ps = [psum(lk, f"row_ps{s}") for s in range(R)]
            tr_ps = [psum(lk, f"tr_ps{s}") for s in (0, 1)]
            hi_in = [sem(f"hi_in{s}") for s in range(R)]
            hot_ready, rows_done, rows_free, all_cols, tr_done, er_ready, er_out = (sem(n) for n in (
                "hot_ready", "rows_done", "rows_free", "all_cols", "tr_done", "er_ready", "er_out"))
            with nc.Block() as block:
                @block.sync
                def _(sp):
                    with sp.Fori(0, NC // R) as i:
                        for s in range(R):
                            sp.wait_ge(rows_free, i * R + s + 1)
                            sp.dma_start(hi_row[s][:], src_hi[ds((i * R + s) * CH, CH)].partition_broadcast(NT)).then_inc(hi_in[s], 16)
                    for b in range(8):
                        sp.wait_ge(er_ready, b + 1)
                        sp.dma_start(es_rows.rearrange("(b r p) -> b r p", b=8, p=P)[b], er[:, b, :]).then_inc(er_out, 16)
                    sp.wait_ge(er_out, 16 * 8)

                @block.scalar
                def _(act):
                    for b in range(8):
                        act.wait_ge(tr_done, b + 1)
                        nc.scalar.activation(er[:, b, :], tr_ps[b % 2][0:TB, 0:P], ACT.Identity,
                                             bias=es_floor[0:TB, 1:2]).then_inc(er_ready, 1)

                @block.gpsimd
                def _(pool):
                    with pool.Fori(0, NC // R) as i:
                        for s in range(R):
                            pool.wait_ge(rows_free, i * R + s + 1)
                            hold(pool, hi_in[s], 16 * i + 16)
                            nc.gpsimd.tensor_scalar(hot[s][:], hi_row[s][:], C["iota_col"][0:NT, :], None,
                                                    ALU.is_equal).then_inc(hot_ready, 1)

                @block.tensor
                def _(pe):
                    with pe.Fori(0, NC // R) as i:
                        for s in range(R):
                            pe.wait_ge(hot_ready, i * R + s + 1)
                            pe.wait_ge(rows_free, i * R + s + 1)
                            for j in range(TPC):
                                last = nc.tensor.matmul(row_ps[s][:, j * P:(j + 1) * P], hot[s][:, j * P:(j + 1) * P], es_lut[:],
                                                        start=True, stop=True)
                            last.then_inc(rows_done, 1)
                    pe.wait_ge(all_cols, 1)
                    for b in range(8):
                        if b >= 2:
                            pe.wait_ge(er_ready, b - 1)
                        nc.tensor.transpose(tr_ps[b % 2][0:TB, 0:P], es_col[:, b * TB:(b + 1) * TB], C["ident"]).then_inc(tr_done, 1)

                @block.vector
                def _(dve):
                    dve.sem_inc(rows_free, R)
                    with dve.Fori(0, NC // R) as i:
                        for s in range(R):
                            dve.wait_ge(rows_done, i * R + s + 1)
                            for j in range(TPC):
                                col = (i * R + s) * TPC + j
                                last = nc.vector.scalar_tensor_tensor(
                                    picked[:, s * TPC + j, :], C["iota_row"], lo_col[:, ds(col, 1)], row_ps[s][:, j * P:(j + 1) * P],
                                    ALU.is_equal, ALU.mult, accum_out=es_col[:, ds(col, 1)])
                            last.then_inc(rows_free, 1)
                    dve.wait_ge(rows_free, NC + R)
                    nc.vector.tensor_scalar(es2_col[:], es_col[:], 0.2, None, ALU.mult).then_inc(all_cols, 1)

        def visit_range(eng, t):
            base = 4 * t
            first = eng.value_load(ranges[:, ds(base, 1)], min_val=0, max_val=ET - VT)
            limit = eng.value_load(ranges[:, ds(base + 1, 1)], min_val=1, max_val=ET - VT + 1)
            shift = eng.value_load(ranges[:, ds(base + 2, 1)], min_val=-ET, max_val=NT * ET)
            return first, limit, shift

        with ExitStack() as pk:
            dst_row = sb(pk, "dst_row", [P, 2 * VE], I32)
            es_row = sb(pk, "es_row", [P, 2 * VE])
            masked = sb(pk, "masked", [P, VE])
            top = sb(pk, "top", [P, 2])
            above = sb(pk, "above", [P, NT])
            tmp = sb(pk, "tmp", [P, 2, NT])
            pq = sb(pk, "pq", [P, 2, NT])
            pqT = sb(pk, "pqT", [NT, 2, P])
            pq_ps = psum(pk, "pq_ps")
            rows_in, rows_used, pk_step, tile_step, fin = (sem(n) for n in ("rows_in", "rows_used", "pk_step", "tile_step", "fin"))
            pq_ready, pq_done, pq_out = sem("pq_ready"), sem("pq_done"), sem("pq_out")
            with nc.Block() as block:
                @block.sync
                def _(sp):
                    with sp.Fori(0, NT) as t:
                        first, limit, shift = visit_range(sp, t)
                        with sp.Fori(first, limit, VT) as at_tile:
                            v = sp.snap(((at_tile + shift) & 0xFFFF) >> (VT.bit_length() - 1))
                            slot = sp.snap((v & 1) * VE)
                            hold(sp, rows_used, v + 1)
                            sp.dma_start(dst_row[:, ds(slot, VE)], a["dst_row"][ds(at_tile * P, VE)].partition_broadcast(P)).then_inc(rows_in, 16)
                            sp.dma_start(es_row[:, ds(slot, VE)], es_rows[ds(at_tile * P, VE)].partition_broadcast(P)).then_inc(rows_in, 16)
                            hold(sp, rows_in, 32 * v + 32)
                    sp.wait_ge(pq_done, 1)
                    sp.dma_start(pq_rows.rearrange("k (t p) -> t k p", p=P), pqT[:]).then_inc(pq_out, 16)
                    sp.wait_ge(pq_out, 17)

                @block.vector
                def _(dve):
                    dve.sem_inc(rows_used, 2)
                    nc.vector.tensor_scalar(above[:], esed[:, :, 0], es_floor[:, 0:1], None, ALU.subtract).then_inc(fin, 1)
                    dve.wait_ge(fin, 1)
                    with dve.Fori(0, NT) as t:
                        first, limit, shift = visit_range(dve, t)
                        nc.vector.tensor_copy(top[:, 0:1], above[:, ds(t, 1)]).then_inc(tile_step, 1)
                        hold(dve, tile_step, 2 * t + 1)
                        with dve.Fori(first, limit, VT) as at_tile:
                            v = dve.snap(((at_tile + shift) & 0xFFFF) >> (VT.bit_length() - 1))
                            slot = dve.snap((v & 1) * VE)
                            dve.wait_ge(rows_in, 32 * v + 32)
                            nc.vector.scalar_tensor_tensor(masked[:], dst_row[:, ds(slot, VE)], C["node_id"][:, ds(t, 1)],
                                                           es_row[:, ds(slot, VE)], ALU.is_equal, ALU.mult).then_inc(rows_used, 1)
                            dve.wait_ge(rows_used, v + 3)
                            nc.vector.tensor_reduce(top[:, 1:2], masked[:], AX.X, ALU.max).then_inc(pk_step, 1)
                            dve.wait_ge(pk_step, 2 * v + 1)
                            nc.vector.tensor_tensor(top[:, 0:1], top[:, 0:1], top[:, 1:2], ALU.max).then_inc(pk_step, 1)
                            hold(dve, pk_step, 2 * v + 2)
                        nc.vector.tensor_copy(peak[:, ds(t, 1)], top[:, 0:1]).then_inc(tile_step, 1)
                        hold(dve, tile_step, 2 * t + 2)
                    steps = Steps(dve, fin, 0)
                    steps.n = 1

                    def step(ins):
                        steps.done(ins)
                        steps.settle()
                    es, ed = esed[:, :, 0], esed[:, :, 1]
                    step(nc.vector.scalar_tensor_tensor(tmp[:, 0, :], peak[:], es_floor[:, 0:1], ed, ALU.add, ALU.add))
                    step(nc.vector.scalar_tensor_tensor(peak[:], tmp[:, 0, :], 0.2, tmp[:, 0, :], ALU.mult, ALU.max))
                    step(nc.vector.tensor_tensor(pq[:, 0, :], ed, peak[:], ALU.subtract))
                    step(nc.vector.scalar_tensor_tensor(pq[:, 1, :], ed, 0.2, peak[:], ALU.mult, ALU.subtract))
                    step(nc.vector.tensor_tensor(tmp[:, 0, :], es, pq[:, 0, :], ALU.add))
                    step(nc.vector.scalar_tensor_tensor(tmp[:, 1, :], es, 0.2, pq[:, 1, :], ALU.mult, ALU.add))
                    step(nc.vector.tensor_tensor(tmp[:, 0, :], tmp[:, 0, :], tmp[:, 1, :], ALU.max))
                    nc.vector.tensor_copy(tmp[:, 1, :], tmp[:, 0, :]).then_inc(pq_ready, 1)
                    dve.wait_ge(pq_done, 1)

                @block.scalar
                def _(act):
                    act.wait_ge(pq_ready, 1)
                    nc.scalar.activation(w_self[:], tmp[:, 1, :], ACT.Exp).then_inc(pq_out, 1)
                    act.wait_ge(pq_ready, 2)
                    nc.scalar.copy(pqT[:].rearrange("t k p -> t (k p)"), pq_ps[0:NT, 0:2 * P]).then_inc(pq_done, 1)

                @block.tensor
                def _(pe):
                    pe.wait_ge(pq_ready, 1)
                    nc.tensor.transpose(pq_ps[0:NT, 0:P], pq[:, 0, :], C["ident"])
                    nc.tensor.transpose(pq_ps[0:NT, P:2 * P], pq[:, 1, :], C["ident"]).then_inc(pq_ready, 1)

        with ExitStack() as ag:
            G = [sb(ag, f"rows{j}", [P, D]) for j in range(VT)]
            idx = sb(ag, "idx", [P, VT], I32)
            argp = sb(ag, "argp", [P, VT, P])
            argq = sb(ag, "argq", [P, VT, P])
            hits = sb(ag, "hits", [P, VT, P])
            ex = sb(ag, "ex", [P, VT, P])
            W = sb(ag, "W", [P, VT, P])
            own = [sb(ag, f"own{s}", [P, D]) for s in (0, 1)]
            xr = [sb(ag, f"xr{s}", [P, D]) for s in (0, 1)]
            pqb = [sb(ag, f"pqb{s}", [P, 2, P]) for s in (0, 1)]
            diag = [sb(ag, f"diag{s}", [P, P]) for s in (0, 1)]
            window = sb(ag, "window", [P, P])
            den = sb(ag, "den", [P, KC, P])
            qd = sb(ag, "qd", [P, KC, P])
            xres = [sb(ag, f"xres{s}", [P, D]) for s in (0, 1)]
            o = sb(ag, "o", [P, D])
            eo = sb(ag, "eo", [P, D])
            res = sb(ag, "res", [P, D])
            x2 = [sb(ag, f"x2{s}", [P, D]) for s in (0, 1)]
            rs = sb(ag, "rs", [P, 1])
            gbias = sb(ag, "gbias", [P, D])
            pbias = sb(ag, "pbias", [1, D])
            zb = sb(ag, "zb", [1, D], BF16)
            den_ps = psum(ag, "den_ps")
            y_ps, acc_ps, s_ps = ([psum(ag, f"{n}{s}") for s in (0, 1)] for n in ("y_ps", "acc_ps", "s_ps"))

            row_in = [sem(f"row_in{j}") for j in range(VT)]
            idx_ready, landed = sem("idx_ready"), sem("landed")
            tile_in = [sem(f"tile_in{s}") for s in (0, 1)]
            x2_out = [sem(f"x2_out{s}") for s in (0, 1)]
            den_step, window_ready = sem("den_step"), sem("window_ready")
            bias_in, z_ready, row_used, arg_ready, ex_ready, w_ready, hits_ready, argq_ready, dve_t = (
                sem(n) for n in ("bias_in", "z_ready", "row_used", "arg_ready", "ex_ready",
                                 "w_ready", "hits_ready", "argq_ready", "dve_t"))
            den_done, diag_ready, acc_done, qd_ready, y_done, eo_in, eo_step, eo_ready, xres_ready, x2_ready = (
                sem(n) for n in ("den_done", "diag_ready", "acc_done", "qd_ready", "y_done",
                                 "eo_in", "eo_step", "eo_ready", "xres_ready", "x2_ready"))
            with nc.Block() as block:
                @block.sync
                def _(sp):
                    sp.dma_start(gbias[:], a["gbias"].partition_broadcast(P)).then_inc(bias_in, 16)
                    sp.dma_start(pbias[:], a["pbias"].rearrange("(o d) -> o d", o=1)).then_inc(bias_in, 16)
                    sp.sem_inc(landed, 2)

                    def own_rows(t, s):
                        sp.wait_ge(x2_ready, t + 1)
                        sp.dma_start(own[s][:], h_rows[ds(t * P, P), :]).then_inc(tile_in[s], 16)
                        sp.dma_start(xr[s][:], a["x"][ds(t * P, P), :]).then_inc(tile_in[s], 16)
                        for k in range(2):
                            sp.dma_start(pqb[s][:, k, :], pq_rows[k, ds(t * P, P)].partition_broadcast(P)).then_inc(tile_in[s], 16)

                    own_rows(0, 0)
                    for t, s, i in tiles(sp):
                        first, limit, shift = visit_range(sp, t)
                        with sp.Fori(first, limit, VT) as at_tile:
                            v = sp.snap(((at_tile + shift) & 0xFFFF) >> (VT.bit_length() - 1))
                            for half in (0, 1):
                                for j in range(half * HT, half * HT + HT):
                                    sp.wait_ge(row_in[j], 16 * v + 16)
                                sp.sem_inc(landed, 1)
                        if not isinstance(t, int):
                            own_rows(t + 1, 1 - s)

                @block.gpsimd
                def _(pool):
                    nc.gpsimd.memset(zb[:], 0.0).then_inc(z_ready, 1)
                    with pool.Fori(0, NT) as t:
                        first, limit, shift = visit_range(pool, t)
                        with pool.Fori(first, limit, VT) as at_tile:
                            v = pool.snap(((at_tile + shift) & 0xFFFF) >> (VT.bit_length() - 1))
                            for half in (0, 1):
                                js = half * HT
                                hold(pool, landed, 2 * v + half + 1)
                                nc.gpsimd.tensor_copy(idx[:, js:js + HT], src_col[:, ds(at_tile + js, HT)]).then_inc(idx_ready, 1)
                                hold(pool, idx_ready, 2 * v + half + 1)
                                for j in range(js, js + HT):
                                    hold(pool, row_used, VT * v + j + 1)
                                    nc.gpsimd.indirect_dma_start(G[j][:], None, h_rows, bass.IndirectOffsetOnAxis(ap=idx[:, j:j + 1], axis=0)).then_inc(row_in[j], 16)

                @block.scalar
                def _(act):
                    for s in (0, 1):
                        act.sem_inc(x2_out[s], 16)
                    act.sem_inc(xres_ready, 1)

                    def residual(t, s, i):
                        hold(act, tile_in[s], 64 * i + 64)
                        nc.scalar.activation(xres[s][:], xr[s][:], ACT.Identity, bias=ln_keep[:, ds(t, 1), 1],
                                             scale=ln_keep[:, ds(t, 1), 0]).then_inc(xres_ready, 1)

                    residual(0, 0, 0)
                    for t, s, i in tiles(act):
                        first, limit, shift = visit_range(act, t)
                        with act.Fori(first, limit, VT) as at_tile:
                            v = act.snap(((at_tile + shift) & 0xFFFF) >> (VT.bit_length() - 1))
                            for half in (0, 1):
                                hs = slice(half * HT, half * HT + HT)
                                act.wait_ge(arg_ready, 2 * v + half + 1)
                                nc.scalar.activation(ex[:, hs, :], argp[:, hs, :], ACT.Exp).then_inc(ex_ready, 1)
                        if not isinstance(t, int):
                            residual(t + 1, 1 - s, i + s)
                        act.wait_ge(eo_in, t + 1)
                        nc.scalar.activation(eo[:], o[:], ACT.Relu, scale=-1.0).then_inc(eo_step, 1)
                        act.wait_ge(eo_step, t + 1)
                        nc.scalar.activation(eo[:], eo[:], ACT.Exp, scale=-1.0).then_inc(eo_ready, 1)
                        act.wait_ge(x2_ready, t + 3)
                        act.dma_start(x2_rows[ds(t * P, P), :], x2[s][:]).then_inc(x2_out[s], 16)
                    act.wait_ge(x2_out[0], 16 * (NT // 2 + 2))
                    act.wait_ge(x2_out[1], 16 * (NT // 2 + 1))

                @block.tensor
                def _(pe):
                    pe.wait_ge(z_ready, 1)
                    pe.wait_ge(bias_in, 32)

                    def denominators(t):
                        for c in range(KC):
                            last = nc.tensor.matmul(den_ps[:, c * P:(c + 1) * P], kb_head[:, c, :], qT[:, c, ds(t * P, P)], start=True, stop=True)
                        last.then_inc(den_done, 1)

                    denominators(0)
                    for t, s, i in tiles(pe):
                        pe.wait_ge(x2_ready, t + 1)
                        pe.wait_ge(qd_ready, t + 1)
                        for c in range(KC):
                            nc.tensor.matmul(y_ps[s][:], qd[:, c, :], fold_w[:, c, :], start=(c == 0), stop=False)
                        nc.tensor.matmul(y_ps[s][:], C["ones_row"][0:1, :], pbias[:], start=False, stop=False)
                        pe.wait_ge(xres_ready, t + 2)
                        nc.tensor.matmul(y_ps[s][:], C["ident"], xres[s][:], start=False, stop=True).then_inc(y_done, 1)
                        if not isinstance(t, int):
                            denominators(t + 1)
                        nc.tensor.matmul(acc_ps[s][:], zb[:, 0:P], zb[:], start=True, stop=False, skip_group_check=True)
                        nc.tensor.matmul(s_ps[s][:, 0:2], zb[:, 0:P], zb[:, 0:2], start=True, stop=False, skip_group_check=True)
                        first, limit, shift = visit_range(pe, t)
                        with pe.Fori(first, limit, VT) as at_tile:
                            v = pe.snap(((at_tile + shift) & 0xFFFF) >> (VT.bit_length() - 1))
                            for j in range(VT):
                                pe.wait_ge(w_ready, VT * v + j + 2)
                                nc.tensor.matmul(s_ps[s][:, 0:1], W[:, j, :], C["ones"], start=False, stop=False, skip_group_check=True)
                                pe.wait_ge(row_in[j], 16 * v + 16)
                                nc.tensor.matmul(acc_ps[s][:], W[:, j, :], G[j][:], start=False, stop=False,
                                                 skip_group_check=True).then_inc(row_used, 1)
                        pe.wait_ge(diag_ready, t + 1)
                        nc.tensor.matmul(s_ps[s][:, 0:1], diag[s][:], C["ones"], start=False, stop=True, skip_group_check=True)
                        pe.wait_ge(tile_in[s], 64 * i + 64)
                        nc.tensor.matmul(acc_ps[s][:], diag[s][:], own[s][:], start=False, stop=True, skip_group_check=True).then_inc(acc_done, 1)

                @block.vector
                def _(dve):
                    dve.sem_inc(row_used, VT)
                    dve.sem_inc(w_ready, 1)
                    dve.sem_inc(x2_ready, 2)
                    dve.wait_ge(bias_in, 32)

                    def queries(t):
                        dve.wait_ge(den_done, t + 1)
                        nc.vector.tensor_scalar(den[:], den_ps[:].rearrange("p (c k) -> p c k", c=KC), 100.0, None, ALU.max).then_inc(den_step, 1)
                        dve.wait_ge(den_step, 2 * t + 1)
                        nc.vector.reciprocal(den[:], den[:]).then_inc(den_step, 1)
                        dve.wait_ge(den_step, 2 * t + 2)
                        nc.vector.tensor_tensor(qd[:], qT[:, :, ds(t * P, P)], den[:], ALU.mult).then_inc(qd_ready, 1)

                    queries(0)
                    for t, s, i in tiles(dve):
                        first, limit, shift = visit_range(dve, t)
                        nc.vector.tensor_scalar(diag[s][:], C["ident"], w_self[:, ds(t, 1)], None, ALU.mult).then_inc(diag_ready, 1)
                        nc.vector.tensor_scalar(window[:], C["iota_row"], C["tile_start"][:, ds(t, 1)], None, ALU.add).then_inc(window_ready, 1)
                        hold(dve, tile_in[s], 64 * i + 64)
                        hold(dve, window_ready, t + 1)
                        with dve.Fori(first, limit, VT) as at_tile:
                            v = dve.snap(((at_tile + shift) & 0xFFFF) >> (VT.bit_length() - 1))
                            for half in (0, 1):
                                slots = range(half * HT, half * HT + HT)
                                for j in slots:
                                    nc.vector.tensor_scalar(argq[:, j, :], pqb[s][:, 1, :], es2_col[:, ds(at_tile + j, 1)], None,
                                                            ALU.add).then_inc(argq_ready, 1)
                                for j in slots:
                                    dve.wait_ge(argq_ready, VT * v + j + 1)
                                    last = nc.vector.scalar_tensor_tensor(argp[:, j, :], pqb[s][:, 0, :], es_col[:, ds(at_tile + j, 1)],
                                                                          argq[:, j, :], ALU.add, ALU.max)
                                last.then_inc(arg_ready, 1)
                                dve.wait_ge(w_ready, VT * v + half * HT + 1)
                                for j in slots:
                                    last = nc.vector.tensor_scalar(hits[:, j, :], window[:], dst_col[:, ds(at_tile + j, 1)], None, ALU.is_equal)
                                last.then_inc(hits_ready, 1)
                                dve.wait_ge(hits_ready, 2 * v + half + 1)
                                dve.wait_ge(ex_ready, 2 * v + half + 1)
                                for j in slots:
                                    dve.wait_ge(row_used, VT * v + j + 1)
                                    nc.vector.scalar_tensor_tensor(W[:, j, :], ex[:, j, :], 3.0, hits[:, j, :], ALU.min, ALU.mult).then_inc(w_ready, 1)
                        if not isinstance(t, int):
                            dve.wait_ge(y_done, t + 1)
                            queries(t + 1)
                        tstep = Steps(dve, dve_t, 3)
                        tstep.round(t)
                        dve.wait_ge(acc_done, t + 1)
                        tstep.done(nc.vector.reciprocal(rs[:], s_ps[s][:, 0:1]))
                        tstep.settle()
                        nc.vector.scalar_tensor_tensor(o[:], acc_ps[s][:], rs[:], gbias[:], ALU.mult, ALU.add).then_inc(eo_in, 1)
                        dve.wait_ge(eo_in, t + 1)
                        dve.wait_ge(y_done, t + 1)
                        tstep.done(nc.vector.scalar_tensor_tensor(res[:], o[:], 0.0, y_ps[s][:], ALU.max, ALU.add))
                        dve.wait_ge(eo_ready, t + 1)
                        tstep.settle()
                        dve.wait_ge(x2_out[s], 16 * i + 16)
                        tstep.done(nc.vector.scalar_tensor_tensor(x2[s][:], eo[:], -1.0, res[:], ALU.add, ALU.add))
                        tstep.settle()
                        dve.sem_inc(x2_ready, 1)

        graph.close()

        with ExitStack() as ex:
            w1 = sb(ex, "w1", [P, NE, KC, F])
            w2 = sb(ex, "w2", [P, NE, FC, D])
            b1 = sb(ex, "b1", [1, NE, F])
            b2 = sb(ex, "b2", [P, NE, D])
            gamma = sb(ex, "gamma", [P, NE, D])
            beta = sb(ex, "beta", [P, NE, D])
            router = sb(ex, "router", [P, KC, NE])
            logits = sb(ex, "logits", [P, NT, NE])
            gates = sb(ex, "gates", [P, 2, NT])
            slot_of = sb(ex, "slot_of", [P, 2, NT], I32)
            token_of = sb(ex, "token_of", [P, P], I32)
            expert_of = sb(ex, "expert_of", [1, ST], I32)
            weights_in = sem("expert_weights_in")

            with ExitStack() as no:
                xb, xf, xfT = ([sb(no, f"{n}{s}", [P, D]) for s in (0, 1)] for n in ("fxb", "fxf", "fxfT"))
                bn, mv, sd = ([sb(no, f"{n}{s}", [P, w]) for s in (0, 1)] for n, w in (("fbn", 6), ("fmv", 2), ("fsd", 2)))
                T_ps, l_ps = ([psum(no, f"{n}{s}") for s in (0, 1)] for n in ("fT_ps", "fl_ps"))
                x_in, xf_out = ([sem(f"{n}{s}") for s in (0, 1)] for n in ("fx_in", "fxf_out"))
                (router_in, bn_ready, mv_ready, var_ready, rstd_ready, xf_ready, T_done, xfT_ready, l_done, l_ready) = (
                    sem("f_" + n) for n in ("router_in", "bn_ready", "mv_ready", "var_ready", "rstd_ready", "xf_ready", "T_done",
                                            "xfT_ready", "l_done", "l_ready"))
                with nc.Block() as block:
                    @block.sync
                    def _(sp):
                        sp.dma_start(router[:], a["router"]).then_inc(router_in, 16)
                        for t, s, i in tiles(sp):
                            sp.wait_ge(xf_ready, t + 1)
                            sp.dma_start(xb[s][:], x2_rows[ds(t * P, P), :]).then_inc(x_in[s], 16)

                    @block.gpsimd
                    def _(pool):
                        for dst, src in ((w1[:], a["w1"]), (w2[:], a["w2"]), (b1[:], a["b1"]), (b2[:], a["b2"].partition_broadcast(P)),
                                         (gamma[:], a["gamma"].partition_broadcast(P)), (beta[:], a["beta"].partition_broadcast(P))):
                            nc.gpsimd.dma_start(dst, src).then_inc(weights_in, 16)
                        for t, s, i in tiles(pool):
                            pool.wait_ge(mv_ready, t + 1)
                            nc.gpsimd.tensor_tensor(sd[s][:, 0:1], mv[s][:, 1:2], C["ln_eps"], ALU.add).then_inc(var_ready, 1)
                            pool.wait_ge(var_ready, t + 1)
                            nc.gpsimd.tensor_tensor(sd[s][:, 1:2], sd[s][:, 0:1], C["minus_half"], ALU.pow).then_inc(rstd_ready, 1)

                    @block.vector
                    def _(dve):
                        dve.sem_inc(xf_ready, 2)

                        def moments(t, s, i):
                            dve.wait_ge(x_in[s], 16 * i + 16)
                            nc.vector.bn_stats(bn[s][:], xb[s][:]).then_inc(bn_ready, 1)
                            hold(dve, bn_ready, t + 1)
                            nc.vector.bn_aggr(mv[s][:], bn[s][:]).then_inc(mv_ready, 1)

                        moments(0, 0, 0)
                        for t, s, i in tiles(dve):
                            if not isinstance(t, int):
                                moments(t + 1, 1 - s, i + s)
                            dve.wait_ge(mv_ready, t + 1)
                            dve.wait_ge(rstd_ready, t + 1)
                            dve.wait_ge(xf_out[s], 16 * i + 16)
                            dve.wait_ge(T_done, t + 1)
                            nc.vector.tensor_scalar(xf[s][:], xb[s][:], mv[s][:, 0:1], sd[s][:, 1:2], ALU.subtract, ALU.mult).then_inc(xf_ready, 1)

                    @block.scalar
                    def _(act):
                        for s in (0, 1):
                            act.sem_inc(xf_out[s], 16)
                        act.sem_inc(l_ready, 2)

                        def turn(t, s):
                            act.wait_ge(xf_ready, t + 3)
                            act.dma_start(xf_rows[ds(t * P, P), :], xf[s][:]).then_inc(xf_out[s], 16)
                            act.wait_ge(T_done, t + 3)
                            act.wait_ge(l_ready, t + 1)
                            nc.scalar.copy(xfT[s][:], T_ps[s][:]).then_inc(xfT_ready, 1)

                        turn(0, 0)
                        for t, s, i in tiles(act):
                            if not isinstance(t, int):
                                turn(t + 1, 1 - s)
                            hold(act, l_done, t + 1)
                            nc.scalar.copy(logits[:, ds(t, 1), :], l_ps[s][:, 0:NE].unsqueeze(1)).then_inc(l_ready, 1)
                        act.wait_ge(xf_out[0], 16 * (NT // 2 + 2))
                        act.wait_ge(xf_out[1], 16 * (NT // 2 + 1))

                    @block.tensor
                    def _(pe):
                        pe.wait_ge(router_in, 16)
                        pe.sem_inc(T_done, 2)
                        pe.sem_inc(xfT_ready, 2)

                        def turn(t, s):
                            pe.wait_ge(xf_ready, t + 3)
                            pe.wait_ge(xfT_ready, t + 1)
                            for c in range(KC):
                                last = nc.tensor.transpose(T_ps[s][:, c * P:(c + 1) * P], xf[s][:, c * P:(c + 1) * P], C["ident"])
                            last.then_inc(T_done, 1)

                        turn(0, 0)
                        for t, s, i in tiles(pe):
                            if not isinstance(t, int):
                                turn(t + 1, 1 - s)
                            pe.wait_ge(xfT_ready, t + 3)
                            pe.wait_ge(l_ready, t + 1)
                            for c in range(KC):
                                last = nc.tensor.matmul(l_ps[s][:, 0:NE], xfT[s][:, c * P:(c + 1) * P], router[:, c, :], start=(c == 0), stop=(c == KC - 1))
                            last.then_inc(l_done, 1)

            with ExitStack() as ro:
                top, first, dif = sb(ro, "top_logit", [P, 2, NT]), sb(ro, "first", [P, NT]), sb(ro, "dif", [P, 2, NT])
                rest, spare = sb(ro, "rest", [P, NT, NE]), sb(ro, "spare", [P, NT, NE])
                pick = sb(ro, "pick", [P, 2, NT, NE])
                picked_by = sb(ro, "picked_by", [P, NT, NE])
                run = [sb(ro, f"run{s}", [P, NT, NE]) for s in (0, 1)]
                end = [sb(ro, f"end{s}", [P, NE]) for s in (0, 1)]
                filled, filled_i = sb(ro, "filled", [P, NE]), sb(ro, "filled_i", [P, NE], I32)
                start = sb(ro, "start_of", [P, NE])
                slot_f, listed_i, part_i = sb(ro, "slot_f", [P, 2, NT]), sb(ro, "listed_i", [P, 2, NT], I32), sb(ro, "part_i", [P, 2, NT], I32)
                hi, lo = sb(ro, "slot_hi", [P, 2, NT]), sb(ro, "slot_lo", [P, 2, NT])
                at_or_past, owner = sb(ro, "at_or_past", [1, ST, NE]), sb(ro, "owner", [1, ST])
                hot_hi, hot_lo = ([sb(ro, f"{n}{k}", [P, P]) for k in (0, 1)] for n in ("hot_hi", "hot_lo"))
                zero16 = sb(ro, "zero16", [P, P], BF16)
                ahead_ps, count_ps, token_ps = psum(ro, "ahead_ps"), psum(ro, "count_ps"), psum(ro, "token_ps")
                r_step, dif_ready, exp_ready, picks_ready, picks_counted, hot_ready, hot_used, zero_ready, tokens_done = (
                    sem("r_" + n) for n in ("step", "dif_ready", "exp_ready", "picks_ready", "picks_counted", "hot_ready", "hot_used",
                                            "zero_ready", "tokens_done"))
                with nc.Block() as block:
                    @block.gpsimd
                    def _(pool):
                        nc.gpsimd.memset(zero16[:], 0.0).then_inc(zero_ready, 1)

                    @block.scalar
                    def _(act):
                        act.wait_ge(dif_ready, 1)
                        nc.scalar.activation(dif[:, 1, :], dif[:, 0, :], ACT.Exp).then_inc(exp_ready, 1)

                    @block.tensor
                    def _(pe):
                        flat = lambda v: v.rearrange("p t e -> p (t e)")
                        pe.wait_ge(picks_ready, 1)
                        nc.tensor.matmul(ahead_ps[:, 0:NT * NE], C["before"], flat(picked_by[:]), start=True, stop=True)
                        nc.tensor.matmul(count_ps[:, 0:NT * NE], C["ones_row"], flat(picked_by[:]), start=True, stop=True).then_inc(picks_counted, 1)
                        pe.wait_ge(zero_ready, 1)
                        nc.tensor.matmul(token_ps[:, 0:P], zero16[:], zero16[:], start=True, stop=False, skip_group_check=True)
                        with pe.Fori(0, NT) as t:
                            for k in (0, 1):
                                pe.wait_ge(hot_ready, 2 * t + k + 1)
                                nc.tensor.matmul(token_ps[:, 0:P], hot_lo[k][:], hot_hi[k][:], start=False, stop=False, skip_group_check=True).then_inc(hot_used, 1)
                        nc.tensor.matmul(token_ps[:, 0:P], zero16[:], zero16[:], start=False, stop=True, skip_group_check=True).then_inc(tokens_done, 1)

                    @block.vector
                    def _(dve):
                        steps = Steps(dve, r_step, 0)
                        dve.sem_inc(hot_used, 2)

                        def step(ins):
                            steps.done(ins)
                            steps.settle()

                        every_expert = lambda v: v.unsqueeze(2).broadcast_to([P, NT, NE])
                        every_tile = lambda v: v.unsqueeze(1).broadcast_to([P, NT, NE])
                        V = nc.vector
                        expert_id = every_tile(C["iota_row"][:, 0:NE])
                        for k, left in ((0, logits), (1, rest)):
                            step(V.tensor_reduce(top[:, k, :], left[:], AX.X, ALU.max))
                            step(V.tensor_tensor(spare[:], left[:], every_expert(top[:, k, :]), ALU.is_equal))
                            step(V.scalar_tensor_tensor(spare[:], spare[:], -100.0, expert_id, ALU.mult, ALU.add))
                            step(V.tensor_reduce(first[:], spare[:], AX.X, ALU.min))
                            step(V.tensor_scalar(first[:], first[:], 100.0, None, ALU.add))
                            step(V.tensor_tensor(pick[:, k], expert_id, every_expert(first[:]), ALU.is_equal))
                            if k == 0:
                                step(V.scalar_tensor_tensor(rest[:], pick[:, 0], -3e38, logits[:], ALU.mult, ALU.add))
                        V.tensor_tensor(dif[:, 0, :], top[:, 1, :], top[:, 0, :], ALU.subtract).then_inc(dif_ready, 1)
                        for k in (0, 1):
                            step(V.tensor_tensor(pick[:, k], pick[:, k], every_expert(C["real"]), ALU.mult))
                        V.tensor_tensor(picked_by[:], pick[:, 0], pick[:, 1], ALU.add).then_inc(picks_ready, 1)
                        dve.wait_ge(exp_ready, 1)
                        step(V.tensor_scalar(first[:], dif[:, 1, :], 1.0, None, ALU.add))
                        step(V.reciprocal(gates[:, 0, :], first[:]))
                        step(V.tensor_tensor(gates[:, 1, :], dif[:, 1, :], gates[:, 0, :], ALU.mult))
                        dve.wait_ge(picks_counted, 1)
                        step(V.tensor_copy(run[0][:], count_ps[:, 0:NT * NE].rearrange("p (t e) -> p t e", e=NE)))
                        side, width = 0, 1
                        while width < NT:
                            V.tensor_copy(run[1 - side][:, 0:width, :], run[side][:, 0:width, :])
                            step(V.tensor_tensor(run[1 - side][:, width:, :], run[side][:, width:, :], run[side][:, 0:NT - width, :], ALU.add))
                            side, width = 1 - side, 2 * width
                        upto, other = run[side], run[1 - side]
                        step(V.tensor_scalar(filled[:], upto[:, NT - 1, :], float(P - 1), None, ALU.add))
                        step(V.tensor_copy(filled_i[:], filled[:]))
                        step(V.tensor_scalar(filled_i[:], filled_i[:], P.bit_length() - 1, None, ALU.arith_shift_right))
                        V.tensor_copy(end[0][:], filled_i[:])
                        step(V.tensor_copy(filled[:], filled_i[:]))
                        eside, width = 0, 1
                        while width < NE:
                            V.tensor_copy(end[1 - eside][:, 0:width], end[eside][:, 0:width])
                            step(V.tensor_tensor(end[1 - eside][:, width:], end[eside][:, width:], end[eside][:, 0:NE - width], ALU.add))
                            eside, width = 1 - eside, 2 * width
                        ends = end[eside]
                        step(V.tensor_tensor(start[:], ends[:], filled[:], ALU.subtract))
                        step(V.tensor_tensor(other[:], upto[:], count_ps[:, 0:NT * NE].rearrange("p (t e) -> p t e", e=NE), ALU.subtract))
                        step(V.tensor_tensor(other[:], other[:], ahead_ps[:, 0:NT * NE].rearrange("p (t e) -> p t e", e=NE), ALU.add))
                        step(V.scalar_tensor_tensor(other[:], every_tile(start[:]), float(P), other[:], ALU.mult, ALU.add))
                        for k in (0, 1):
                            step(V.tensor_tensor(spare[:], pick[:, k], other[:], ALU.mult))
                            step(V.tensor_reduce(slot_f[:, k, :], spare[:], AX.X, ALU.add))
                        step(V.tensor_copy(slot_of[:], slot_f[:]))
                        step(V.tensor_tensor(slot_f[:], slot_f[:], C["past_end"].unsqueeze(1).broadcast_to([P, 2, NT]), ALU.add))
                        step(V.tensor_copy(listed_i[:], slot_f[:]))
                        step(V.tensor_scalar(part_i[:], listed_i[:], P.bit_length() - 1, None, ALU.arith_shift_right))
                        step(V.tensor_copy(hi[:], part_i[:]))
                        step(V.tensor_scalar(part_i[:], listed_i[:], P - 1, None, ALU.bitwise_and))
                        step(V.tensor_copy(lo[:], part_i[:]))
                        step(V.tensor_tensor(at_or_past[:], C["iota_row"][0:1, 0:ST].unsqueeze(2).broadcast_to([1, ST, NE]),
                                             ends[0:1, :].unsqueeze(1).broadcast_to([1, ST, NE]), ALU.is_ge))
                        step(V.tensor_reduce(owner[:], at_or_past[:], AX.X, ALU.add))
                        step(V.tensor_scalar(owner[:], owner[:], float(NE - 1), None, ALU.min))
                        step(V.tensor_copy(expert_of[:], owner[:]))
                        with dve.Fori(0, NT) as t:
                            for k in (0, 1):
                                dve.wait_ge(hot_used, 2 * t + k + 1)
                                V.tensor_scalar(hot_hi[k][:], C["iota_row"], hi[:, k, ds(t, 1)], None, ALU.is_equal)
                                V.tensor_scalar(hot_lo[k][:], C["iota_row"], lo[:, k, ds(t, 1)], C["node_id"][:, ds(t, 1)],
                                                ALU.is_equal, ALU.mult).then_inc(hot_ready, 1)
                        dve.wait_ge(tokens_done, 1)
                        step(V.tensor_copy(token_of[:], token_ps[:, 0:P]))

            with ExitStack() as ep:
                two = lambda name, shape, dt=F32: [sb(ep, f"{name}{s}", shape, dt) for s in (0, 1)]
                rows, rowsT, hid, hidT = two("xs", [P, D]), two("xsT", [P, D]), two("hid", [P, F]), two("hidT", [P, F])
                z0, z, zn, zg, y = two("z0", [P, D]), two("z", [P, D]), two("zn", [P, D]), two("zg", [P, D]), two("y", [P, D])
                idx2, zbn, zmv, zsd = two("idx2", [P, 1], I32), two("zbn", [P, 6]), two("zmv", [P, 2]), two("zsd", [P, 2])
                T_ps, hT_ps = psum(ep, "xT_ps"), psum(ep, "hT_ps")
                hid_ps, o_ps = ([psum(ep, f"{n}{s}") for s in (0, 1)] for n in ("hid_ps", "o_ps"))
                rows_in, y_out = ([sem(f"{n}{s}") for s in (0, 1)] for n in ("xs_in", "y_out"))
                (idx_copied, T_done, T_ready, hid_done, hid_ready, hT_done, hT_ready, o_done, z0_ready, z_ready, zbn_ready, zmv_ready,
                 zvar_ready, zsd_ready, zn_ready, zg_ready, y_ready) = (sem("e_" + n) for n in (
                     "idx_copied", "T_done", "T_ready", "hid_done", "hid_ready", "hT_done", "hT_ready", "o_done", "z0_ready", "z_ready",
                     "zbn_ready", "zmv_ready", "zvar_ready", "zsd_ready", "zn_ready", "zg_ready", "y_ready"))

                def expert(eng, t):
                    return eng.value_load(expert_of[:, ds(t, 1)], min_val=0, max_val=NE - 1)

                with nc.Block() as block:
                    @block.sync
                    def _(sp):
                        for s in (0, 1):
                            sp.sem_inc(y_out[s], 16)
                        for t, s, i in tiles(sp, ST):
                            sp.wait_ge(y_ready, t + 1)
                            sp.dma_start(y_rows[ds(t * P, P), :], y[s][:]).then_inc(y_out[s], 16)
                        sp.wait_ge(y_out[0], 16 * (ST // 2 + 2))
                        sp.wait_ge(y_out[1], 16 * (ST // 2 + 1))

                    @block.gpsimd
                    def _(pool):
                        pool.wait_ge(weights_in, 16 * 6)

                        def gather(t, s):
                            hold(pool, T_done, t + 1)
                            hold(pool, z0_ready, t + 1)
                            nc.gpsimd.tensor_copy(idx2[s][:], token_of[:, ds(t, 1)]).then_inc(idx_copied, 1)
                            hold(pool, idx_copied, t + 1)
                            nc.gpsimd.indirect_dma_start(rows[s][:], None, xf_rows, bass.IndirectOffsetOnAxis(ap=idx2[s][:, 0:1], axis=0)).then_inc(rows_in[s], 16)

                        def base(t, s, i):
                            e = expert(pool, t)
                            pool.wait_ge(rows_in[s], 16 * i + 16)
                            pool.wait_ge(z_ready, t + 1)
                            nc.gpsimd.tensor_tensor(z0[s][:], rows[s][:], b2[:, ds(e, 1), :].rearrange("p o d -> p (o d)"), ALU.add).then_inc(z0_ready, 1)

                        pool.sem_inc(z0_ready, 2)
                        gather(0, 0)
                        gather(1, 1)
                        base(0, 0, 0)
                        for t, s, i in tiles(pool, ST):
                            if not isinstance(t, int):
                                gather(t + 2, s)
                                base(t + 1, 1 - s, i + s)
                            pool.wait_ge(zmv_ready, t + 1)
                            nc.gpsimd.tensor_tensor(zsd[s][:, 0:1], zmv[s][:, 1:2], C["ffn_eps"], ALU.add).then_inc(zvar_ready, 1)
                            pool.wait_ge(zvar_ready, t + 1)
                            nc.gpsimd.tensor_tensor(zsd[s][:, 1:2], zsd[s][:, 0:1], C["minus_half"], ALU.pow).then_inc(zsd_ready, 1)
                        pool.wait_ge(rows_in[1], 16 * (ST // 2 + 1))

                    @block.scalar
                    def _(act):
                        def turned(t, s):
                            act.wait_ge(T_done, t + 3)
                            act.wait_ge(hid_done, t + 1)
                            nc.scalar.copy(rowsT[s][:], T_ps[:]).then_inc(T_ready, 1)

                        turned(0, 0)
                        for t, s, i in tiles(act, ST):
                            act.wait_ge(hid_done, t + 3)
                            act.wait_ge(hT_done, t + 1)
                            nc.scalar.activation(hid[s][:], hid_ps[s][:, 0:F], ACT.Relu).then_inc(hid_ready, 1)
                            if not isinstance(t, int):
                                turned(t + 1, 1 - s)
                            act.wait_ge(hT_done, t + 3)
                            act.wait_ge(o_done, t + 1)
                            nc.scalar.copy(hidT[s][:], hT_ps[:, 0:F]).then_inc(hT_ready, 1)

                    @block.tensor
                    def _(pe):
                        pe.wait_ge(weights_in, 16 * 6)
                        for one in (T_done, hid_done, hT_done, o_done):
                            pe.sem_inc(one, 2)

                        def turn(t, s, i):
                            pe.wait_ge(rows_in[s], 16 * i + 16)
                            for c in range(KC):
                                last = nc.tensor.transpose(T_ps[:, c * P:(c + 1) * P], rows[s][:, c * P:(c + 1) * P], C["ident"])
                            last.then_inc(T_done, 1)

                        def hidden(t, s):
                            e = expert(pe, t)
                            pe.wait_ge(T_ready, t + 1)
                            for c in range(KC):
                                nc.tensor.matmul(hid_ps[s][:, 0:F], rowsT[s][:, c * P:(c + 1) * P], w1[:, ds(e, 1), c, :].rearrange("p o f -> p (o f)"),
                                                 start=(c == 0), stop=False)
                            nc.tensor.matmul(hid_ps[s][:, 0:F], C["ones_row"][0:1, :], b1[:, ds(e, 1), :].rearrange("p o f -> p (o f)"),
                                             start=False, stop=True).then_inc(hid_done, 1)

                        turn(0, 0, 0)
                        hidden(0, 0)
                        for t, s, i in tiles(pe, ST):
                            if not isinstance(t, int):
                                turn(t + 1, 1 - s, i + s)
                            pe.wait_ge(hid_ready, t + 1)
                            for f in range(FC):
                                last = nc.tensor.transpose(hT_ps[:, f * P:(f + 1) * P], hid[s][:, f * P:(f + 1) * P], C["ident"])
                            last.then_inc(hT_done, 1)
                            if not isinstance(t, int):
                                hidden(t + 1, 1 - s)
                            e = expert(pe, t)
                            pe.wait_ge(hT_ready, t + 1)
                            pe.wait_ge(z_ready, t + 1)
                            for f in range(FC):
                                last = nc.tensor.matmul(o_ps[s][:], hidT[s][:, f * P:(f + 1) * P], w2[:, ds(e, 1), f, :].rearrange("p o d -> p (o d)"),
                                                        start=(f == 0), stop=(f == FC - 1))
                            last.then_inc(o_done, 1)

                    @block.vector
                    def _(dve):
                        dve.wait_ge(weights_in, 16 * 6)
                        dve.sem_inc(z_ready, 2)
                        for t, s, i in tiles(dve, ST):
                            e = expert(dve, t)
                            dve.wait_ge(o_done, t + 3)
                            dve.wait_ge(z0_ready, t + 3)
                            nc.vector.tensor_tensor(z[s][:], o_ps[s][:], z0[s][:], ALU.add).then_inc(z_ready, 1)
                            hold(dve, z_ready, t + 3)
                            nc.vector.bn_stats(zbn[s][:], z[s][:]).then_inc(zbn_ready, 1)
                            hold(dve, zbn_ready, t + 1)
                            nc.vector.bn_aggr(zmv[s][:], zbn[s][:]).then_inc(zmv_ready, 1)
                            dve.wait_ge(zmv_ready, t + 1)
                            dve.wait_ge(zsd_ready, t + 1)
                            nc.vector.tensor_scalar(zn[s][:], z[s][:], zmv[s][:, 0:1], zsd[s][:, 1:2], ALU.subtract, ALU.mult).then_inc(zn_ready, 1)
                            dve.wait_ge(zn_ready, t + 1)
                            nc.vector.tensor_tensor(zg[s][:], zn[s][:], gamma[:, ds(e, 1), :].rearrange("p o d -> p (o d)"), ALU.mult).then_inc(zg_ready, 1)
                            dve.wait_ge(zg_ready, t + 1)
                            dve.wait_ge(y_out[s], 16 * i + 16)
                            nc.vector.tensor_tensor(y[s][:], zg[s][:], beta[:, ds(e, 1), :].rearrange("p o d -> p (o d)"), ALU.add).then_inc(y_ready, 1)

            with ExitStack() as co:
                xb, ya, yb, part, ob = ([sb(co, f"{n}{s}", [P, D]) for s in (0, 1)] for n in ("cx", "ya", "yb", "part", "ob"))
                idx3 = [sb(co, f"idx3{s}", [P, 2], I32) for s in (0, 1)]
                x_in, o_out = ([sem(f"{n}{s}") for s in (0, 1)] for n in ("cx_in", "co_out"))
                y_in = [[sem(f"y_in{s}{k}") for k in (0, 1)] for s in (0, 1)]
                idx_copied, part_ready, out_ready = sem("c_idx_copied"), sem("c_part_ready"), sem("c_out_ready")
                with nc.Block() as block:
                    @block.sync
                    def _(sp):
                        for t, s, i in tiles(sp):
                            sp.wait_ge(out_ready, t + 1)
                            sp.dma_start(xb[s][:], x2_rows[ds(t * P, P), :]).then_inc(x_in[s], 16)

                    @block.gpsimd
                    def _(pool):
                        for t, s, i in tiles(pool):
                            hold(pool, out_ready, t + 1)
                            nc.gpsimd.tensor_copy(idx3[s][:], slot_of[:, :, ds(t, 1)].rearrange("p k o -> p (k o)")).then_inc(idx_copied, 1)
                            hold(pool, idx_copied, t + 1)
                            for k, rows in ((0, ya), (1, yb)):
                                nc.gpsimd.indirect_dma_start(rows[s][:], None, y_rows, bass.IndirectOffsetOnAxis(ap=idx3[s][:, k:k + 1], axis=0)).then_inc(y_in[s][k], 16)

                    @block.vector
                    def _(dve):
                        dve.sem_inc(out_ready, 2)
                        for t, s, i in tiles(dve):
                            dve.wait_ge(x_in[s], 16 * i + 16)
                            dve.wait_ge(y_in[s][0], 16 * i + 16)
                            nc.vector.scalar_tensor_tensor(part[s][:], ya[s][:], gates[:, 0, ds(t, 1)], xb[s][:], ALU.mult, ALU.add).then_inc(part_ready, 1)
                            dve.wait_ge(part_ready, t + 1)
                            dve.wait_ge(y_in[s][1], 16 * i + 16)
                            dve.wait_ge(o_out[s], 16 * i + 16)
                            nc.vector.scalar_tensor_tensor(ob[s][:], yb[s][:], gates[:, 1, ds(t, 1)], part[s][:], ALU.mult, ALU.add).then_inc(out_ready, 1)

                    @block.scalar
                    def _(act):
                        for s in (0, 1):
                            act.sem_inc(o_out[s], 16)
                        for t, s, i in tiles(act):
                            act.wait_ge(out_ready, t + 3)
                            act.dma_start(out[ds(t * P, P), :], ob[s][:]).then_inc(o_out[s], 16)
                        act.wait_ge(o_out[0], 16 * (NT // 2 + 2))
                        act.wait_ge(o_out[1], 16 * (NT // 2 + 1))


def lay_out(inputs):
    f = lambda n: np.asarray(inputs[n])
    pad = lambda v, n, c: np.concatenate([v, np.full((n - v.shape[0],) + v.shape[1:], c, v.dtype)])
    rows = lambda w: np.ascontiguousarray(w.reshape(-1, P, w.shape[-1]).transpose(1, 0, 2))
    src, dst = pad(f("src"), EP, 0), pad(f("dst"), EP, NO_NODE)
    temp = f("L0_mix_temperature").reshape(KC, 2)
    return {
        "consts": const_layout()[0],
        "x": pad(f("x"), NP, 0),
        "src_col": np.ascontiguousarray(src.reshape(ET, P).T), "dst_col": np.ascontiguousarray(dst.reshape(ET, P).T),
        "src_lin": src.reshape(ROWP, -1), "dst_lin": dst.reshape(ROWP, -1), "dst_row": dst,
        "wg": rows(f("L0_gnn_W").T), "w_nat": rows(f("L0_gnn_W")),
        "avec": rows(np.stack([f("L0_gnn_a_src"), f("L0_gnn_a_dst")], 1)),
        "gbias": f("L0_gnn_bias"), "pbias": f("L0_mix_bproj"),
        "wqkv": rows(f("L0_mix_Wqkv").T), "wproj": rows(f("L0_mix_Wproj").T),
        "temp": np.ascontiguousarray(np.repeat(temp, 64, axis=1).T),
        "router": rows(f("L0_ffn_router_w")),
        "w1": np.ascontiguousarray(f("L0_ffn_w1").reshape(NE, KC, P, F).transpose(2, 0, 1, 3)),
        "w2": np.ascontiguousarray(f("L0_ffn_w2").reshape(NE, FC, P, D).transpose(2, 0, 1, 3)),
        "b1": f("L0_ffn_b1")[None],
        "b2": f("L0_ffn_b2"), "gamma": f("L0_ffn_gamma"), "beta": f("L0_ffn_beta"),
    }


def kernel(**inputs):
    import concourse.bacc as _bacc
    from concourse.bass_utils import run_bass_kernel_spmd as _run

    nc = _bacc.Bacc("TRN2", target_bir_lowering=False, num_devices=1)
    arrays = {f"in_{n}": v for n, v in lay_out(inputs).items()}
    a = {n[3:]: nc.dram_tensor(n, v.shape, mybir.dt.from_np(v.dtype), kind="ExternalInput").ap() for n, v in arrays.items()}
    out = nc.dram_tensor("out", (NP, D), F32, kind="ExternalOutput").ap()
    gps_layer(nc, a, out)
    return _run(nc, [arrays], core_ids=[0]).results[0]["out"][:N]
```

```python
from contextlib import ExitStack

import numpy as np

import concourse.bass as bass
from concourse import mybir

F32 = mybir.dt.float32
BF16 = mybir.dt.bfloat16
I32 = mybir.dt.int32
U32 = mybir.dt.uint32
ALU = mybir.AluOpType
ACT = mybir.ActivationFunctionType
AX = mybir.AxisListType
ds = bass.ds

P = 128
N, D, E = 6250, 512, 100000
NT = -(-N // P)
NP = NT * P
CH = 512
TPC = CH // P
VT = 8
HT = VT // 2
VE = VT * P
EP = 100 * VE
ET = EP // P
NC = EP // CH
assert EP >= E + VE
KC = D // P
HD = P // 2
NH = 2 * KC
NE, F = 8, 256
FC = F // P
ST = 2 * N // P + NE
assert ST % 2 == 1 and ST + 2 <= P
LN_EPS, FFN_EPS = 1e-5, 1e-6
NO_NODE = 9999
ROWP = EP // VE
TB = ET // 8


def const_layout():
    parts = {
        "ident": np.eye(P),
        "iota_row": np.tile(np.arange(P), (P, 1)),
        "iota_col": np.arange(P)[:, None],
        "minus_col": -np.arange(P)[:, None],
        "node_id": np.arange(NT)[None, :] * P + np.arange(P)[:, None],
        "tile_start": np.tile(np.arange(NT) * P, (P, 1)),
        "same_head": np.kron(np.eye(2), np.ones((64, 64))),
        "ones": np.ones((P, 1)),
        "head_of_row": np.kron(np.eye(2 * KC), np.ones((HD, 1))).reshape(KC, P, 2 * KC).transpose(1, 0, 2).reshape(P, -1),
        "rows_of_head": np.pad(np.kron(np.eye(2 * KC), np.ones((1, HD))), ((0, P - 2 * KC), (0, 0))),
        "ones_row": np.ones((P, P)),
        "minus_half": np.full((P, 1), -0.5),
        "ln_eps": np.full((P, 1), LN_EPS),
        "ffn_eps": np.full((P, 1), FFN_EPS),
        "tile_base": np.arange(P)[:, None] * P,
        "edge_tile_id": np.tile(np.arange(ET), (P, 1)),
        "before": np.triu(np.ones((P, P)), 1),
        "real": (np.arange(NT)[None, :] * P + np.arange(P)[:, None] < N) * 1.0,
        "past_end": (np.arange(NT)[None, :] * P + np.arange(P)[:, None] >= N) * float(P * P),
    }
    at, out = {}, 0
    for name, a in parts.items():
        at[name] = (out, out + a.shape[1])
        out += a.shape[1]
    return np.concatenate([parts[n] for n in parts], 1).astype(np.float32), at


def tiles(eng, n=NT, r=2):
    assert n % r == 1
    with eng.Fori(0, n // r) as i:
        for s in range(r):
            yield r * i + s, s, i
    yield n - 1, 0, n // r


def tiles_behind(eng, n=NT):
    yield 0, 0, 0, None
    with eng.Fori(0, n // 2) as i:
        yield 2 * i + 1, 1, i, (2 * i, 0, i)
        yield 2 * i + 2, 0, i + 1, (2 * i + 1, 1, i)


class Steps:

    def __init__(self, eng, sem, k):
        self.eng, self.sem, self.k, self.base, self.n = eng, sem, k, 0, 0

    def round(self, r):
        assert self.n in (0, self.k), (self.n, self.k)
        self.base, self.n = r * self.k, 0

    def done(self, ins):
        self.n += 1
        ins.then_inc(self.sem, 1)

    def settle(self):
        self.eng.wait_ge(self.sem, self.base + self.n)


def gps_layer(nc, a, out):
    _, at = const_layout()
    dram = lambda name, shape, dt=F32: nc.dram_tensor(name, shape, dt).ap()
    h_rows = dram("h_rows", [NP, D])
    src_hi = dram("src_hi", [EP])
    pair_rows = dram("pair_rows", [2, EP])
    lo_hi = dram("lo_hi", [2, ET])
    ranges_d = dram("ranges_d", [NT, 4], I32)
    pq_rows = dram("pq_rows", [2, NP])
    x2_rows = dram("x2_rows", [NP, D])
    xf_rows = dram("xf_rows", [NP, D])
    y_rows = dram("y_rows", [ST * P, D])

    with ExitStack() as whole:
        def sem(name):
            return whole.enter_context(nc.semaphore(name))

        def sb(scope, name, shape, dt=F32):
            return scope.enter_context(nc.sbuf_tensor(name, shape, dt))

        def psum(scope, name, shape=(P, D), dt=F32):
            return scope.enter_context(nc.psum_tensor(name, list(shape), dt))

        held = {}

        def hold(eng, s, value):
            name = str(eng.engine)
            if name not in held:
                held[name] = sem(f"held_{len(held)}")
            eng.wait_ge(s, value)
            eng.sem_inc(held[name], 1)

        cst = sb(whole, "cst", list(a["consts"].shape))
        C = {n: cst[:, lo:hi] for n, (lo, hi) in at.items()}

        graph = whole.enter_context(ExitStack())
        qT = sb(graph, "qT", [P, KC, NP])
        src_col = sb(graph, "src_col", [P, ET], I32)
        dst_col = sb(graph, "dst_col", [P, ET])
        lo_col = sb(graph, "lo_col", [P, ET])
        es_col = sb(graph, "es_col", [P, ET])
        es2_col = sb(graph, "es2_col", [P, ET])
        esed = sb(graph, "esed", [P, NT, 2])
        ln_keep = sb(graph, "ln_keep", [P, NT, 2])
        k_head = sb(graph, "k_head", [P, KC, NH])
        fold_w = sb(graph, "fold_w", [P, KC, D])
        es_lut = sb(graph, "es_lut", [NT, P])
        ranges = sb(graph, "ranges", [1, NT * 4], I32)
        es_floor = sb(graph, "es_floor", [P, 2])
        peak = sb(graph, "peak", [P, NT])
        w_self = sb(graph, "w_self", [P, NT])

        with ExitStack() as sc:
            wqkv = sb(sc, "wqkv", [P, KC, 3 * D])
            wproj = sb(sc, "wproj", [P, KC, D])
            temp = sb(sc, "temp", [P, KC])
            u = sb(sc, "u", [P, KC, 2])
            pj = sc.enter_context(ExitStack())
            wg = sb(pj, "wg", [P, KC, D])
            ps = ExitStack()
            w_nat = sb(ps, "w_nat", [P, KC, D])
            avec = sb(ps, "avec", [P, KC, 2])
            dst_i = sb(ps, "dst_i", [P, ET], I32)
            lin_i = sb(ps, "lin_i", [ROWP, EP // ROWP], I32)
            lin_f = sb(ps, "lin_f", [ROWP, EP // ROWP])
            lin_d = sb(ps, "lin_d", [ROWP, EP // ROWP])
            lohi_sb = sb(ps, "lohi_sb", [ROWP, 2, VT])
            lohi_bc = sb(ps, "lohi_bc", [NT, 2, ET])
            rtmp = sb(ps, "rtmp", [NT, ET])
            rout = sb(ps, "rout", [NT, 4])
            rout_i = sb(ps, "rout_i", [NT, 4], I32)
            loaded = sem("setup_loaded")
            ints = sem("setup_ints")
            saved = sem("setup_saved")
            r_loaded = sem("range_loaded")
            tri = sem("range_offsets")
            with ps:
                u_ps = psum(ps, "u_ps")
                off_ps = psum(ps, "off_ps")
                u_done = sem("u_done")
                with nc.Block() as block:
                    @block.sync
                    def _(sp):
                        for dst, src in ((cst[:], a["consts"]), (wg[:], a["wg"]), (w_nat[:], a["w_nat"]),
                                         (wqkv[:], a["wqkv"]), (wproj[:], a["wproj"]), (avec[:], a["avec"]),
                                         (temp[:], a["temp"]), (src_col[:], a["src_col"]),
                                         (dst_i[:], a["dst_col"]), (lin_i[:], a["dst_lin"])):
                            sp.dma_start(dst, src).then_inc(loaded, 16)
                        sp.wait_ge(ints, 4)
                        for k in range(2):
                            sp.dma_start(lo_hi[k].rearrange("(p c) -> p c", c=VT), lohi_sb[:, k, :]).then_inc(saved, 16)
                        sp.dma_start(lin_i[:], a["src_lin"]).then_inc(loaded, 16)
                        sp.wait_ge(saved, 32)
                        sp.dma_start(lohi_bc[:], lo_hi.partition_broadcast(NT)).then_inc(r_loaded, 16)
                        sp.dma_start(pair_rows[0].rearrange("(p c) -> p c", p=ROWP), lin_d[:]).then_inc(saved, 16)
                        sp.wait_ge(ints, 6)
                        sp.dma_start(src_hi.rearrange("(p c) -> p c", p=ROWP), lin_f[:]).then_inc(saved, 16)
                        sp.wait_ge(ints, 24)
                        sp.dma_start(ranges_d, rout_i[:]).then_inc(saved, 16)
                        sp.wait_ge(saved, 80)
                        sp.dma_start(ranges[:], ranges_d.rearrange("(o t) c -> o (t c)", o=1)).then_inc(r_loaded, 16)
                        sp.wait_ge(r_loaded, 32)

                    @block.tensor
                    def _(pe):
                        pe.wait_ge(loaded, 160)
                        for k in range(KC):
                            for j in range(KC):
                                last = nc.tensor.matmul(u_ps[:, 2 * k:2 * k + 2], w_nat[:, j, k * P:(k + 1) * P],
                                                        avec[:, j, :], start=(j == 0), stop=(j == KC - 1))
                        last.then_inc(u_done, 1)
                        pe.wait_ge(ints, 20)
                        nc.tensor.matmul(off_ps[0:NT, 0:1], C["before"][0:NT, 0:NT], rout[:, 1:2],
                                         start=True, stop=True).then_inc(tri, 1)

                    @block.vector
                    def _(dve):
                        step = Steps(dve, ints, 0)
                        dve.wait_ge(loaded, 160)
                        lin3 = lin_i[:].rearrange("p (c e) -> p c e", c=VT)
                        step.done(nc.vector.tensor_reduce(lohi_sb[:, 0, :], lin3, AX.X, ALU.min))
                        step.done(nc.vector.tensor_reduce(lohi_sb[:, 1, :], lin3, AX.X, ALU.max))
                        step.done(nc.vector.tensor_copy(dst_col[:], dst_i[:]))
                        step.done(nc.vector.tensor_copy(lin_d[:], lin_i[:]))
                        dve.wait_ge(loaded, 176)
                        step.settle()
                        step.done(nc.vector.tensor_scalar(lin_i[:], lin_i[:], 7, None, ALU.arith_shift_right))
                        step.settle()
                        step.done(nc.vector.tensor_copy(lin_f[:], lin_i[:]))
                        step.done(nc.vector.tensor_scalar(dst_i[:], src_col[:], 127, None, ALU.bitwise_and))
                        step.settle()
                        step.done(nc.vector.tensor_copy(lo_col[:], dst_i[:]))
                        dve.wait_ge(r_loaded, 16)
                        base = C["tile_base"][0:NT, :]
                        cid = C["edge_tile_id"][0:NT, :]
                        step.done(nc.vector.tensor_scalar(rtmp[:], lohi_bc[:, 0, :], base, float(P - 1),
                                                          ALU.subtract, ALU.is_le))
                        step.settle()
                        step.done(nc.vector.scalar_tensor_tensor(rtmp[:], lohi_bc[:, 1, :], base, rtmp[:],
                                                                 ALU.is_ge, ALU.mult))
                        step.settle()
                        step.done(nc.vector.scalar_tensor_tensor(lohi_bc[:, 0, :], rtmp[:], -1000.0, cid,
                                                                 ALU.mult, ALU.add))
                        step.done(nc.vector.scalar_tensor_tensor(lohi_bc[:, 1, :], cid, 1.0, rtmp[:],
                                                                 ALU.add, ALU.mult))
                        step.settle()
                        step.done(nc.vector.tensor_reduce(rout[:, 0:1], lohi_bc[:, 0, :], AX.X, ALU.min))
                        step.done(nc.vector.tensor_reduce(rout[:, 1:2], lohi_bc[:, 1, :], AX.X, ALU.max))
                        step.settle()
                        step.done(nc.vector.tensor_scalar(rout[:, 0:1], rout[:, 0:1], 1000.0, float(ET - VT),
                                                          ALU.add, ALU.min))
                        step.settle()
                        step.done(nc.vector.scalar_tensor_tensor(rout[:, 1:2], rout[:, 1:2], float(VT - 1), rout[:, 0:1],
                                                                 ALU.add, ALU.subtract))
                        step.settle()
                        step.done(nc.vector.tensor_copy(rout_i[:, 1:2], rout[:, 1:2]))
                        step.settle()
                        step.done(nc.vector.tensor_scalar(rout_i[:, 3:4], rout_i[:, 1:2], VT.bit_length() - 1, None, ALU.arith_shift_right))
                        step.settle()
                        step.done(nc.vector.tensor_copy(rout[:, 2:3], rout_i[:, 3:4]))
                        step.settle()
                        step.done(nc.vector.tensor_scalar(rout[:, 1:2], rout[:, 2:3], 1.0, None, ALU.max))
                        assert step.n == 20
                        dve.wait_ge(tri, 1)
                        step.settle()
                        step.done(nc.vector.scalar_tensor_tensor(rout[:, 2:3], off_ps[0:NT, 0:1], float(VT), rout[:, 0:1],
                                                                 ALU.mult, ALU.subtract))
                        step.done(nc.vector.scalar_tensor_tensor(rout[:, 3:4], rout[:, 1:2], float(VT), rout[:, 0:1],
                                                                 ALU.mult, ALU.add))
                        step.settle()
                        step.done(nc.vector.tensor_scalar(rout[:, 1:2], rout[:, 3:4], float(1 - VT), None, ALU.add))
                        step.settle()
                        step.done(nc.vector.tensor_copy(rout_i[:], rout[:]))
                        dve.wait_ge(u_done, 1)
                        nc.vector.tensor_copy(u[:].rearrange("p c o -> p (c o)"), u_ps[:, 0:2 * KC]).then_inc(ints, 1)

            with pj:
                xb = [sb(pj, f"xb{s}", [P, D]) for s in (0, 1)]
                xn = [sb(pj, f"xn{s}", [P, D]) for s in (0, 1)]
                xnT = [sb(pj, f"xnT{s}", [P, KC, P]) for s in (0, 1)]
                hb = [sb(pj, f"hb{s}", [P, D]) for s in (0, 1)]
                bn = [sb(pj, f"bn{s}", [P, 6]) for s in (0, 1)]
                mv = [sb(pj, f"mv{s}", [P, 2]) for s in (0, 1)]
                sd = [sb(pj, f"sd{s}", [P, 2]) for s in (0, 1)]
                T_ps = psum(pj, "T_ps")
                h_ps, e_ps = ([psum(pj, f"{n}{s}") for s in (0, 1)] for n in ("h_ps", "e_ps"))
                x_in = [sem(f"x_in{s}") for s in (0, 1)]
                h_out = [sem(f"h_out{s}") for s in (0, 1)]
                x_free, xn_ready, rstd_ready, mv_ready, bn_ready = (sem(n) for n in (
                    "x_free", "xn_ready", "rstd_ready", "mv_ready", "bn_ready"))
                T_ready, xnT_ready, xnT_kept, h_done, hb_ready, h_free = (sem(n) for n in (
                    "T_ready", "xnT_ready", "xnT_kept", "h_done", "hb_ready", "h_free"))

                with nc.Block() as block:
                    @block.sync
                    def _(sp):
                        sp.sem_inc(x_free, 2)
                        for t, s, i in tiles(sp):
                            sp.wait_ge(x_free, t + 1)
                            sp.dma_start(xb[s][:], a["x"][ds(t * P, P), :]).then_inc(x_in[s], 16)

                    @block.gpsimd
                    def _(pool):
                        for t, s, i in tiles(pool):
                            pool.wait_ge(mv_ready, t + 1)
                            nc.gpsimd.tensor_tensor(sd[s][:, 0:1], mv[s][:, 1:2], C["ln_eps"], ALU.add).then_inc(rstd_ready, 1)
                            pool.wait_ge(rstd_ready, 2 * t + 1)
                            nc.gpsimd.tensor_tensor(sd[s][:, 1:2], sd[s][:, 0:1], C["minus_half"], ALU.pow).then_inc(rstd_ready, 1)

                    @block.vector
                    def _(dve):
                        dve.sem_inc(h_free, 2)

                        def norm(t, s, i):
                            dve.wait_ge(x_in[s], 16 * i + 16)
                            nc.vector.bn_stats(bn[s][:], xb[s][:]).then_inc(bn_ready, 1)
                            hold(dve, bn_ready, t + 1)
                            nc.vector.bn_aggr(mv[s][:], bn[s][:]).then_inc(mv_ready, 1)
                            dve.wait_ge(rstd_ready, 2 * t + 2)
                            dve.wait_ge(mv_ready, t + 1)
                            dve.wait_ge(T_ready, t + 1)
                            nc.vector.tensor_scalar(xn[s][:], xb[s][:], mv[s][:, 0:1], sd[s][:, 1:2],
                                                    ALU.subtract, ALU.mult).then_inc(xn_ready, 1)
                            nc.vector.tensor_scalar(ln_keep[:, ds(t, 1), 0], sd[s][:, 1:2], 1.0, None, ALU.add)
                            nc.vector.scalar_tensor_tensor(ln_keep[:, ds(t, 1), 1], mv[s][:, 0:1], -1.0, sd[s][:, 1:2],
                                                           ALU.mult, ALU.mult).then_inc(x_free, 1)

                        norm(0, 0, 0)
                        for t, s, i in tiles(dve):
                            if not isinstance(t, int):
                                norm(t + 1, 1 - s, i + s)
                            dve.wait_ge(h_done, t + 1)
                            dve.wait_ge(h_out[s], 16 * i + 16)
                            nc.vector.tensor_copy(hb[s][:], h_ps[s][:]).then_inc(hb_ready, 1)
                            nc.vector.tensor_copy(esed[:, ds(t, 1), :], e_ps[s][:, 0:2].unsqueeze(1)).then_inc(h_free, 1)

                    @block.scalar
                    def _(act):
                        for s in (0, 1):
                            act.sem_inc(h_out[s], 16)

                        def turned(t, s):
                            act.wait_ge(T_ready, t + 3)
                            act.wait_ge(h_free, t + 1)
                            nc.scalar.copy(xnT[s][:].rearrange("p c k -> p (c k)"), T_ps[:]).then_inc(xnT_ready, 1)
                            hold(act, xnT_ready, t + 1)
                            nc.scalar.copy(qT[:, :, ds(t * P, P)], xnT[s][:]).then_inc(xnT_kept, 1)

                        turned(0, 0)
                        for t, s, i in tiles(act):
                            if not isinstance(t, int):
                                turned(t + 1, 1 - s)
                            act.wait_ge(hb_ready, t + 1)
                            act.dma_start(h_rows[ds(t * P, P), :], hb[s][:]).then_inc(h_out[s], 16)
                        act.wait_ge(xnT_kept, NT)
                        act.wait_ge(h_out[0], 16 * (NT // 2 + 2))
                        act.wait_ge(h_out[1], 16 * (NT // 2 + 1))

                    @block.tensor
                    def _(pe):
                        pe.sem_inc(T_ready, 2)

                        def transposes(t, s):
                            pe.wait_ge(xn_ready, t + 1)
                            for c in range(KC):
                                last = nc.tensor.transpose(T_ps[:, c * P:(c + 1) * P], xn[s][:, c * P:(c + 1) * P], C["ident"])
                            last.then_inc(T_ready, 1)

                        transposes(0, 0)
                        for t, s, i in tiles(pe):
                            pe.wait_ge(xnT_ready, t + 1)
                            pe.wait_ge(h_free, t + 1)
                            for c in range(KC):
                                nc.tensor.matmul(h_ps[s][:], xnT[s][:, c, :], wg[:, c, :], start=(c == 0), stop=(c == KC - 1))
                            if not isinstance(t, int):
                                transposes(t + 1, 1 - s)
                            for c in range(KC):
                                last = nc.tensor.matmul(e_ps[s][:, 0:2], xnT[s][:, c, :], u[:, c, :], start=(c == 0), stop=(c == KC - 1))
                            last.then_inc(h_done, 1)

                lows = sb(pj, "lows", [P, 2])
                low_step, low_pe = sem("low_step"), sem("low_pe")
                with nc.Block() as block:
                    @block.vector
                    def _(dve):
                        nc.vector.tensor_reduce(lows[:, 0:1], esed[:, :, 0], AX.X, ALU.min).then_inc(low_step, 1)
                        dve.wait_ge(low_step, 1)
                        nc.vector.tensor_scalar(lows[:, 1:2], lows[:, 0:1], -1.0, None, ALU.mult).then_inc(low_step, 1)
                        dve.wait_ge(low_pe, 1)
                        nc.vector.tensor_copy(es_lut[:], T_ps[0:NT, 0:P])
                        dve.wait_ge(low_step, 3)
                        nc.vector.tensor_scalar(es_floor[:, 0:1], lows[:, 0:1], -1.0, None, ALU.mult)
                        nc.vector.tensor_copy(es_floor[:, 1:2], lows[:, 0:1])

                    @block.gpsimd
                    def _(pool):
                        pool.wait_ge(low_step, 2)
                        nc.gpsimd.partition_all_reduce(lows[:, 0:1], lows[:, 1:2], P, bass.bass_isa.ReduceOp.max).then_inc(low_step, 1)

                    @block.tensor
                    def _(pe):
                        nc.tensor.transpose(T_ps[0:NT, 0:P], esed[:, :, 0], C["ident"]).then_inc(low_pe, 1)

            R = 4
            SPREAD = 64
            with ExitStack() as lk:
                hi_row = [sb(lk, f"hi_row{s}", [SPREAD, CH]) for s in range(R)]
                hot = [sb(lk, f"hot{s}", [NT, CH]) for s in range(R)]
                picked = sb(lk, "picked", [P, R * TPC, P])
                er = sb(lk, "er", [TB, 8, P])
                row_ps = [psum(lk, f"row_ps{s}") for s in range(R)]
                tr_ps = [psum(lk, f"tr_ps{s}") for s in (0, 1)]
                hi_in = [sem(f"hi_in{s}") for s in range(R)]
                hot_ready = [sem(f"hot_ready{s}") for s in range(R)]
                apart, rows_done, rows_free, all_cols, tr_done, er_ready, er_out = (sem(n) for n in (
                    "apart", "rows_done", "rows_free", "all_cols", "tr_done", "er_ready", "er_out"))
                with nc.Block() as block:
                    @block.sync
                    def _(sp):
                        for s in range(R):
                            sp.sem_inc(hot_ready[s], 1)
                        sp.sem_inc(rows_done, R)
                        with sp.Fori(0, NC // R) as i:
                            for s in range(R):
                                sp.wait_ge(hot_ready[s], i + 1)
                                sp.dma_start(hi_row[s][:], src_hi[ds((i * R + s) * CH, CH)].partition_broadcast(SPREAD)).then_inc(hi_in[s], 16)
                        for b in range(8):
                            sp.wait_ge(er_ready, b + 1)
                            sp.dma_start(pair_rows[1].rearrange("(b r p) -> b r p", b=8, p=P)[b], er[:, b, :]).then_inc(er_out, 16)
                        sp.wait_ge(er_out, 16 * 8)

                    @block.scalar
                    def _(act):
                        with act.Fori(0, NC // R) as i:
                            for s in range(1, R, 2):
                                act.wait_ge(rows_done, i * R + s + 1)
                                act.wait_ge(hi_in[s], 16 * i + 16)
                                nc.scalar.activation(hot[s][:], hi_row[s][0:NT, :], ACT.Abs, bias=C["minus_col"][0:NT, :]).then_inc(apart, 1)
                                act.wait_ge(apart, i * (R // 2) + s // 2 + 1)
                                nc.scalar.activation(hot[s][:], hot[s][:], ACT.Relu, bias=C["ones"][0:NT, :], scale=-1.0).then_inc(hot_ready[s], 1)
                        for b in range(8):
                            act.wait_ge(tr_done, b + 1)
                            nc.scalar.activation(er[:, b, :], tr_ps[b % 2][0:TB, 0:P], ACT.Identity,
                                                 bias=es_floor[0:TB, 1:2]).then_inc(er_ready, 1)

                    @block.gpsimd
                    def _(pool):
                        with pool.Fori(0, NC // R) as i:
                            for s in range(0, R, 2):
                                pool.wait_ge(rows_done, i * R + s + 1)
                                hold(pool, hi_in[s], 16 * i + 16)
                                nc.gpsimd.tensor_scalar(hot[s][:], hi_row[s][0:NT, :], C["iota_col"][0:NT, :], None,
                                                        ALU.is_equal).then_inc(hot_ready[s], 1)

                    @block.tensor
                    def _(pe):
                        with pe.Fori(0, NC // R) as i:
                            for s in range(R):
                                pe.wait_ge(hot_ready[s], i + 2)
                                pe.wait_ge(rows_free, i * R + s + 1)
                                for j in range(TPC):
                                    last = nc.tensor.matmul(row_ps[s][:, j * P:(j + 1) * P], hot[s][:, j * P:(j + 1) * P], es_lut[:],
                                                            start=True, stop=True)
                                last.then_inc(rows_done, 1)
                        pe.wait_ge(all_cols, 1)
                        for b in range(8):
                            if b >= 2:
                                pe.wait_ge(er_ready, b - 1)
                            nc.tensor.transpose(tr_ps[b % 2][0:TB, 0:P], es_col[:, b * TB:(b + 1) * TB], C["ident"]).then_inc(tr_done, 1)

                    @block.vector
                    def _(dve):
                        dve.sem_inc(rows_free, R)
                        with dve.Fori(0, NC // R) as i:
                            for s in range(R):
                                dve.wait_ge(rows_done, i * R + s + R + 1)
                                for j in range(TPC):
                                    col = (i * R + s) * TPC + j
                                    last = nc.vector.scalar_tensor_tensor(
                                        picked[:, s * TPC + j, :], C["iota_row"], lo_col[:, ds(col, 1)], row_ps[s][:, j * P:(j + 1) * P],
                                        ALU.is_equal, ALU.mult, accum_out=es_col[:, ds(col, 1)])
                                last.then_inc(rows_free, 1)
                        dve.wait_ge(rows_free, NC + R)
                        nc.vector.tensor_scalar(es2_col[:], es_col[:], 0.2, None, ALU.mult).then_inc(all_cols, 1)

            def visit_range(eng, t):
                base = 4 * t
                first = eng.value_load(ranges[:, ds(base, 1)], min_val=0, max_val=ET - VT)
                limit = eng.value_load(ranges[:, ds(base + 1, 1)], min_val=1, max_val=ET - VT + 1)
                shift = eng.value_load(ranges[:, ds(base + 2, 1)], min_val=-ET, max_val=NT * ET)
                return first, limit, shift

            Q = 4
            QE = VE // Q
            with ExitStack() as pk:
                pair = [sb(pk, f"pair{h}", [P, 2, QE]) for h in range(Q)]
                xnT = [sb(pk, f"pxnT{s}", [P, KC, P]) for s in (0, 1)]
                kb = [sb(pk, f"kb{s}", [P, D]) for s in (0, 1)]
                vb = [sb(pk, f"vb{s}", [P, D]) for s in (0, 1)]
                zb = sb(pk, "zb16", [1, D], BF16)
                abT = sb(pk, "abT", [P, KC, P])
                ks_sb = sb(pk, "ks_sb", [P, KC])
                k_ps, v_ps, q_ps, kv_ps, ks_ps = (psum(pk, n) for n in ("k_ps", "v_ps", "q_ps", "kv_ps", "ks_ps"))
                xnT_ready, k_done, v_done, q_done, kb_ready, vb_ready, q_ready, kv_done, zeroed = (sem("p_" + n) for n in (
                    "xnT_ready", "k_done", "v_done", "q_done", "kb_ready", "vb_ready", "q_ready", "kv_done", "zeroed"))
                masked = sb(pk, "masked", [P, VE])
                top = sb(pk, "top", [P, 2])
                above = sb(pk, "above", [P, NT])
                tmp = sb(pk, "tmp", [P, 2, NT])
                pq = sb(pk, "pq", [P, 2, NT])
                pqT = sb(pk, "pqT", [NT, 2, P])
                pq_ps = psum(pk, "pq_ps")
                rows_in = [sem(f"rows_in{h}") for h in range(Q)]
                rows_used, pk_step, tile_step, fin = (sem(n) for n in ("rows_used", "pk_step", "tile_step", "fin"))
                pq_ready, pq_done, pq_out = sem("pq_ready"), sem("pq_done"), sem("pq_out")
                with nc.Block() as block:
                    @block.sync
                    def _(sp):
                        with sp.Fori(0, NT) as t:
                            first, limit, shift = visit_range(sp, t)
                            with sp.Fori(first, limit, VT) as at_tile:
                                v = sp.snap(((at_tile + shift) & 0xFFFF) >> (VT.bit_length() - 1))
                                for h in range(Q):
                                    edges = ds(at_tile * P + h * QE, QE)
                                    sp.wait_ge(rows_used, Q * v + h + 1)
                                    sp.dma_start(pair[h][:], pair_rows[:, edges].partition_broadcast(P)).then_inc(rows_in[h], 16)
                        sp.wait_ge(pq_done, 1)
                        sp.dma_start(pq_rows.rearrange("k (t p) -> t k p", p=P), pqT[:]).then_inc(pq_out, 16)
                        sp.wait_ge(pq_out, 17)

                    @block.vector
                    def _(dve):
                        dve.sem_inc(rows_used, Q)
                        nc.vector.tensor_scalar(above[:], esed[:, :, 0], es_floor[:, 0:1], None, ALU.subtract).then_inc(fin, 1)
                        dve.wait_ge(fin, 1)
                        with dve.Fori(0, NT) as t:
                            first, limit, shift = visit_range(dve, t)
                            nc.vector.tensor_copy(top[:, 0:1], above[:, ds(t, 1)]).then_inc(tile_step, 1)
                            hold(dve, tile_step, 2 * t + 1)
                            with dve.Fori(first, limit, VT) as at_tile:
                                v = dve.snap(((at_tile + shift) & 0xFFFF) >> (VT.bit_length() - 1))
                                for h in range(Q):
                                    dve.wait_ge(rows_in[h], 16 * v + 16)
                                    nc.vector.scalar_tensor_tensor(masked[:, h * QE:(h + 1) * QE], pair[h][:, 0, :], C["node_id"][:, ds(t, 1)],
                                                                   pair[h][:, 1, :], ALU.is_equal, ALU.mult).then_inc(rows_used, 1)
                                dve.wait_ge(rows_used, Q * v + 2 * Q)
                                nc.vector.tensor_reduce(top[:, 1:2], masked[:], AX.X, ALU.max).then_inc(pk_step, 1)
                                dve.wait_ge(pk_step, 2 * v + 1)
                                nc.vector.tensor_tensor(top[:, 0:1], top[:, 0:1], top[:, 1:2], ALU.max).then_inc(pk_step, 1)
                                hold(dve, pk_step, 2 * v + 2)
                            nc.vector.tensor_copy(peak[:, ds(t, 1)], top[:, 0:1]).then_inc(tile_step, 1)
                            hold(dve, tile_step, 2 * t + 2)
                        steps = Steps(dve, fin, 0)
                        steps.n = 1

                        def step(ins):
                            steps.done(ins)
                            steps.settle()
                        es, ed = esed[:, :, 0], esed[:, :, 1]
                        step(nc.vector.scalar_tensor_tensor(tmp[:, 0, :], peak[:], es_floor[:, 0:1], ed, ALU.add, ALU.add))
                        step(nc.vector.scalar_tensor_tensor(peak[:], tmp[:, 0, :], 0.2, tmp[:, 0, :], ALU.mult, ALU.max))
                        step(nc.vector.tensor_tensor(pq[:, 0, :], ed, peak[:], ALU.subtract))
                        step(nc.vector.scalar_tensor_tensor(pq[:, 1, :], ed, 0.2, peak[:], ALU.mult, ALU.subtract))
                        step(nc.vector.tensor_tensor(tmp[:, 0, :], es, pq[:, 0, :], ALU.add))
                        step(nc.vector.scalar_tensor_tensor(tmp[:, 1, :], es, 0.2, pq[:, 1, :], ALU.mult, ALU.add))
                        step(nc.vector.tensor_tensor(tmp[:, 0, :], tmp[:, 0, :], tmp[:, 1, :], ALU.max))
                        nc.vector.tensor_copy(tmp[:, 1, :], tmp[:, 0, :]).then_inc(pq_ready, 1)
                        dve.wait_ge(pq_done, 1)

                    @block.scalar
                    def _(act):
                        def fetch(t, s):
                            hold(act, kb_ready, t + 1)
                            hold(act, vb_ready, t + 1)
                            hold(act, q_ready, t + 1)
                            nc.scalar.copy(xnT[s][:], qT[:, :, ds(t * P, P)]).then_inc(xnT_ready, 1)

                        for one in (kb_ready, vb_ready, q_ready):
                            act.sem_inc(one, 2)
                        fetch(0, 0)
                        for t, s, i in tiles(act):
                            act.wait_ge(k_done, t + 1)
                            act.wait_ge(kv_done, t + 1)
                            nc.scalar.activation(kb[s][:], k_ps[:], ACT.Relu).then_inc(kb_ready, 1)
                            if not isinstance(t, int):
                                fetch(t + 1, 1 - s)
                            act.wait_ge(v_done, t + 1)
                            nc.scalar.copy(vb[s][:], v_ps[:]).then_inc(vb_ready, 1)
                            hold(act, q_done, t + 1)
                            hold(act, xnT_ready, t + 1)
                            nc.scalar.activation(qT[:, :, ds(t * P, P)], q_ps[:].rearrange("p (c k) -> p c k", c=KC), ACT.Relu).then_inc(q_ready, 1)
                        act.wait_ge(q_ready, NT + 2)
                        act.wait_ge(pq_ready, 1)
                        nc.scalar.activation(w_self[:], tmp[:, 1, :], ACT.Exp).then_inc(pq_out, 1)
                        act.wait_ge(pq_ready, 2)
                        nc.scalar.copy(pqT[:].rearrange("t k p -> t (k p)"), pq_ps[0:NT, 0:2 * P]).then_inc(pq_done, 1)

                    @block.gpsimd
                    def _(pool):
                        nc.gpsimd.memset(zb[:], 0.0).then_inc(zeroed, 1)

                    @block.tensor
                    def _(pe):
                        pe.sem_inc(kv_done, 2)
                        pe.wait_ge(zeroed, 1)
                        nc.tensor.matmul(kv_ps[:], zb[:, 0:P], zb[:], start=True, stop=False, skip_group_check=True)
                        nc.tensor.matmul(ks_ps[:, 0:KC], zb[:, 0:P], zb[:, 0:KC], start=True, stop=False, skip_group_check=True)
                        for t, s, i in tiles(pe):
                            pe.wait_ge(xnT_ready, t + 1)
                            pe.wait_ge(kb_ready, t + 2)
                            for c in range(KC):
                                last = nc.tensor.matmul(k_ps[:], xnT[s][:, c, :], wqkv[:, c, D:2 * D], start=(c == 0), stop=(c == KC - 1))
                            last.then_inc(k_done, 1)
                            pe.wait_ge(vb_ready, t + 2)
                            for c in range(KC):
                                last = nc.tensor.matmul(v_ps[:], xnT[s][:, c, :], wqkv[:, c, 2 * D:3 * D], start=(c == 0), stop=(c == KC - 1))
                            last.then_inc(v_done, 1)
                            pe.wait_ge(q_ready, t + 2)
                            for j in range(KC):
                                for c in range(KC):
                                    last = nc.tensor.matmul(q_ps[:, j * P:(j + 1) * P], wqkv[:, c, j * P:(j + 1) * P], xnT[s][:, c, :],
                                                            start=(c == 0), stop=(c == KC - 1))
                            last.then_inc(q_done, 1)
                            pe.wait_ge(kb_ready, t + 3)
                            pe.wait_ge(vb_ready, t + 3)
                            for c in range(KC):
                                cs = slice(c * P, (c + 1) * P)
                                nc.tensor.matmul(kv_ps[:, cs], vb[s][:, cs], kb[s][:, cs], start=False, stop=False, skip_group_check=True)
                                last = nc.tensor.matmul(ks_ps[:, c:c + 1], kb[s][:, cs], C["ones"], start=False, stop=False, skip_group_check=True)
                            last.then_inc(kv_done, 1)
                        nc.tensor.matmul(kv_ps[:], zb[:, 0:P], zb[:], start=False, stop=True, skip_group_check=True)
                        nc.tensor.matmul(ks_ps[:, 0:KC], zb[:, 0:P], zb[:, 0:KC], start=False, stop=True, skip_group_check=True)
                        pe.wait_ge(pq_ready, 1)
                        nc.tensor.transpose(pq_ps[0:NT, 0:P], pq[:, 0, :], C["ident"])
                        nc.tensor.transpose(pq_ps[0:NT, P:2 * P], pq[:, 1, :], C["ident"]).then_inc(pq_ready, 1)

                fold_dve, fold_pe = sem("fold_dve"), sem("fold_pe")
                with nc.Block() as block:
                    @block.vector
                    def _(dve):
                        for c in range(KC):
                            nc.vector.scalar_tensor_tensor(abT[:, c, :], kv_ps[:, c * P:(c + 1) * P], temp[:, c:c + 1],
                                                           C["same_head"], ALU.mult, ALU.mult).then_inc(fold_dve, 1)
                        nc.vector.tensor_copy(ks_sb[:], ks_ps[:, 0:KC]).then_inc(fold_dve, 1)
                        dve.wait_ge(fold_dve, KC + 1)
                        for c in range(KC):
                            nc.vector.tensor_scalar(k_head[:, c, :], C["head_of_row"][:, c * NH:(c + 1) * NH], ks_sb[:, c:c + 1], None, ALU.mult)
                        for c in range(KC):
                            dve.wait_ge(fold_pe, c + 1)
                            nc.vector.tensor_copy(fold_w[:, c, :], (k_ps, v_ps, q_ps, pq_ps)[c][:])

                    @block.tensor
                    def _(pe):
                        for c in range(KC):
                            pe.wait_ge(fold_dve, c + 1)
                            nc.tensor.matmul((k_ps, v_ps, q_ps, pq_ps)[c][:], abT[:, c, :], wproj[:, c, :],
                                             start=True, stop=True).then_inc(fold_pe, 1)

        with ExitStack() as ag:
            G = [sb(ag, f"rows{j}", [P, D]) for j in range(VT)]
            idx = sb(ag, "idx", [P, VT], I32)
            argp = sb(ag, "argp", [P, VT, P])
            argq = sb(ag, "argq", [P, VT, P])
            cap = sb(ag, "cap", [P, VT, P])
            W = sb(ag, "W", [P, 2, 1 + HT, P])
            w_of = lambda j: W[:, j // HT, 1 + j % HT, :]
            w_sum = W[:, 0, 0, :]
            w_total = [sb(ag, f"w_total{s}", [P, P]) for s in (0, 1)]
            own = [sb(ag, f"own{s}", [P, D]) for s in (0, 1)]
            xr = [sb(ag, f"xr{s}", [P, D]) for s in (0, 1)]
            pqb = [sb(ag, f"pqb{s}", [P, 2, P]) for s in (0, 1)]
            diag = [sb(ag, f"diag{s}", [P, P]) for s in (0, 1)]
            window = sb(ag, "window", [P, P])
            den = sb(ag, "den", [NH, P])
            qd = [sb(ag, f"qd{s}", [P, KC, P]) for s in (0, 1)]
            xres = [sb(ag, f"xres{s}", [P, D]) for s in (0, 1)]
            o = sb(ag, "o", [P, D])
            eo = sb(ag, "eo", [P, D])
            res = sb(ag, "res", [P, D])
            x2 = [sb(ag, f"x2{s}", [P, D]) for s in (0, 1)]
            rs = sb(ag, "rs", [P, 1])
            gbias = sb(ag, "gbias", [P, D])
            pbias = sb(ag, "pbias", [1, D])
            zb = sb(ag, "zb", [1, D], BF16)
            den_ps, spread_ps = psum(ag, "den_ps"), psum(ag, "spread_ps")
            y_ps, acc_ps, s_ps = ([psum(ag, f"{n}{s}") for s in (0, 1)] for n in ("y_ps", "acc_ps", "s_ps"))

            row_in = [sem(f"row_in{j}") for j in range(VT)]
            idx_ready, landed = sem("idx_ready"), sem("landed")
            tile_in = [sem(f"tile_in{s}") for s in (0, 1)]
            x2_out = [sem(f"x2_out{s}") for s in (0, 1)]
            den_step, den_inverse, spread_done, summed, sum_zeroed, total_ready = (sem(n) for n in ("den_step", "den_inverse", "spread_done", "summed", "sum_zeroed", "total_ready"))
            bias_in, z_ready, row_used, argp_ready, arg_ready, w_ready, argq_ready, dve_t = (
                sem(n) for n in ("bias_in", "z_ready", "row_used", "argp_ready", "arg_ready",
                                 "w_ready", "argq_ready", "dve_t"))
            den_done, diag_ready, acc_done, qd_ready, y_done, eo_in, eo_step, eo_ready, xres_ready, x2_ready = (
                sem(n) for n in ("den_done", "diag_ready", "acc_done", "qd_ready", "y_done",
                                 "eo_in", "eo_step", "eo_ready", "xres_ready", "x2_ready"))
            with nc.Block() as block:
                @block.sync
                def _(sp):
                    sp.dma_start(gbias[:], a["gbias"].partition_broadcast(P)).then_inc(bias_in, 16)
                    sp.dma_start(pbias[:], a["pbias"].rearrange("(o d) -> o d", o=1)).then_inc(bias_in, 16)
                    sp.sem_inc(landed, 2)

                    def own_rows(t, s):
                        sp.wait_ge(acc_done, t + 1)
                        sp.dma_start(own[s][:], h_rows[ds(t * P, P), :]).then_inc(tile_in[s], 16)
                        sp.dma_start(xr[s][:], a["x"][ds(t * P, P), :]).then_inc(tile_in[s], 16)
                        for k in range(2):
                            sp.dma_start(pqb[s][:, k, :], pq_rows[k, ds(t * P, P)].partition_broadcast(P)).then_inc(tile_in[s], 16)

                    sp.sem_inc(acc_done, 2)
                    for t, s, i, last in tiles_behind(sp):
                        own_rows(t, s)
                        first, limit, shift = visit_range(sp, t)
                        with sp.Fori(first, limit, VT) as at_tile:
                            v = sp.snap(((at_tile + shift) & 0xFFFF) >> (VT.bit_length() - 1))
                            for half in (0, 1):
                                for j in range(half * HT, half * HT + HT):
                                    sp.wait_ge(row_in[j], 16 * v + 16)
                                sp.sem_inc(landed, 1)

                @block.gpsimd
                def _(pool):
                    nc.gpsimd.memset(zb[:], 0.0).then_inc(z_ready, 1)
                    for t, s, i in tiles(pool):
                        first, limit, shift = visit_range(pool, t)
                        with pool.Fori(first, limit, VT) as at_tile:
                            v = pool.snap(((at_tile + shift) & 0xFFFF) >> (VT.bit_length() - 1))
                            for half in (0, 1):
                                js = half * HT
                                hold(pool, landed, 2 * v + half + 1)
                                nc.gpsimd.tensor_copy(idx[:, js:js + HT], src_col[:, ds(at_tile + js, HT)]).then_inc(idx_ready, 1)
                                hold(pool, idx_ready, 2 * v + half + 1)
                                for j in range(js, js + HT):
                                    hold(pool, row_used, VT * v + j + 1)
                                    nc.gpsimd.indirect_dma_start(G[j][:], None, h_rows, bass.IndirectOffsetOnAxis(ap=idx[:, j:j + 1], axis=0)).then_inc(row_in[j], 16)

                @block.scalar
                def _(act):
                    act.sem_inc(xres_ready, 1)

                    def residual(t, s, i):
                        hold(act, tile_in[s], 64 * i + 64)
                        nc.scalar.activation(xres[s][:], xr[s][:], ACT.Identity, bias=ln_keep[:, ds(t, 1), 1],
                                             scale=ln_keep[:, ds(t, 1), 0]).then_inc(xres_ready, 1)

                    def finish(t, s, i):
                        act.wait_ge(eo_in, t + 1)
                        nc.scalar.activation(eo[:], eo[:], ACT.Exp).then_inc(eo_ready, 1)
                        act.wait_ge(x2_ready, t + 3)
                        act.dma_start(x2_rows[ds(t * P, P), :], x2[s][:]).then_inc(x2_out[s], 16)

                    for s in (0, 1):
                        act.sem_inc(x2_out[s], 16)

                    for t, s, i, last_tile in tiles_behind(act):
                        residual(t, s, i)
                        first, limit, shift = visit_range(act, t)
                        with act.Fori(first, limit, VT) as at_tile:
                            v = act.snap(((at_tile + shift) & 0xFFFF) >> (VT.bit_length() - 1))
                            for half in (0, 1):
                                for j in range(half * HT, half * HT + HT):
                                    last = nc.scalar.activation(argq[:, j, :], pqb[s][:, 1, :], ACT.Identity, bias=es2_col[:, ds(at_tile + j, 1)])
                                last.then_inc(argq_ready, 1)
                            for half in (0, 1):
                                hs = slice(half * HT, half * HT + HT)
                                act.wait_ge(row_used, VT * v + half * HT + HT)
                                act.wait_ge(summed, 2 * v + half + 1)
                                act.wait_ge(arg_ready, 2 * v + half + 1)
                                nc.scalar.activation(W[:, half, 1:, :], argp[:, hs, :], ACT.Exp).then_inc(w_ready, 1)
                        if last_tile:
                            finish(*last_tile)
                    finish(NT - 1, 0, NT // 2)
                    act.wait_ge(x2_out[0], 16 * (NT // 2 + 2))
                    act.wait_ge(x2_out[1], 16 * (NT // 2 + 1))

                @block.tensor
                def _(pe):
                    pe.wait_ge(z_ready, 1)
                    pe.wait_ge(bias_in, 32)

                    def denominators(t):
                        for c in range(KC):
                            last = nc.tensor.matmul(den_ps[0:NH, 0:P], k_head[:, c, :], qT[:, c, ds(t * P, P)], start=(c == 0), stop=(c == KC - 1))
                        last.then_inc(den_done, 1)

                    def spread(t):
                        pe.wait_ge(den_inverse, t + 1)
                        for c in range(KC):
                            last = nc.tensor.matmul(spread_ps[:, c * P:(c + 1) * P], C["rows_of_head"][0:NH, c * P:(c + 1) * P], den[:], start=True, stop=True)
                        last.then_inc(spread_done, 1)

                    denominators(0)
                    spread(0)
                    for t, s, i in tiles(pe):
                        first, limit, shift = visit_range(pe, t)
                        if not isinstance(t, int):
                            pe.wait_ge(den_step, t + 1)
                            denominators(t + 1)
                        pe.wait_ge(x2_ready, t + 1)
                        nc.tensor.matmul(acc_ps[s][:], zb[:, 0:P], zb[:], start=True, stop=False, skip_group_check=True)
                        with pe.Fori(first, limit, VT) as at_tile:
                            v = pe.snap(((at_tile + shift) & 0xFFFF) >> (VT.bit_length() - 1))
                            for j in range(VT):
                                if j % HT == 0:
                                    pe.wait_ge(w_ready, 2 * v + j // HT + 3)
                                pe.wait_ge(row_in[j], 16 * v + 16)
                                nc.tensor.matmul(acc_ps[s][:], w_of(j), G[j][:], start=False, stop=False,
                                                 skip_group_check=True).then_inc(row_used, 1)
                        pe.wait_ge(diag_ready, t + 1)
                        pe.wait_ge(total_ready, t + 1)
                        nc.tensor.matmul(s_ps[s][:, 0:1], w_total[s][:], C["ones"], start=True, stop=False)
                        nc.tensor.matmul(s_ps[s][:, 0:1], diag[s][:], C["ones"], start=False, stop=True)
                        pe.wait_ge(tile_in[s], 64 * i + 64)
                        nc.tensor.matmul(acc_ps[s][:], diag[s][:], own[s][:], start=False, stop=True, skip_group_check=True).then_inc(acc_done, 1)
                        pe.wait_ge(qd_ready, t + 1)
                        for c in range(KC):
                            nc.tensor.matmul(y_ps[s][:], qd[s][:, c, :], fold_w[:, c, :], start=(c == 0), stop=False)
                        nc.tensor.matmul(y_ps[s][:], C["ones_row"][0:1, :], pbias[:], start=False, stop=False)
                        pe.wait_ge(xres_ready, t + 2)
                        nc.tensor.matmul(y_ps[s][:], C["ident"], xres[s][:], start=False, stop=True).then_inc(y_done, 1)
                        if not isinstance(t, int):
                            spread(t + 1)

                @block.vector
                def _(dve):
                    dve.sem_inc(row_used, VT)
                    dve.sem_inc(w_ready, 2)
                    dve.sem_inc(summed, 2)
                    dve.sem_inc(y_done, 2)
                    dve.sem_inc(spread_done, 1)
                    dve.sem_inc(x2_ready, 2)
                    dve.wait_ge(bias_in, 32)

                    def inverses(t):
                        dve.wait_ge(den_done, t + 1)
                        dve.wait_ge(spread_done, t + 1)
                        nc.vector.tensor_scalar(den[:], den_ps[0:NH, 0:P], 100.0, None, ALU.max).then_inc(den_step, 1)
                        dve.wait_ge(den_step, t + 1)
                        nc.vector.reciprocal(den[:], den[:]).then_inc(den_inverse, 1)

                    def queries(t, s):
                        hold(dve, spread_done, t + 2)
                        hold(dve, y_done, t + 1)
                        nc.vector.tensor_tensor(qd[s][:], qT[:, :, ds(t * P, P)], spread_ps[:].rearrange("p (c k) -> p c k", c=KC), ALU.mult).then_inc(qd_ready, 1)

                    def finish(t, s, i):
                        tstep = Steps(dve, dve_t, 3)
                        tstep.round(t)
                        dve.wait_ge(acc_done, t + 3)
                        tstep.done(nc.vector.reciprocal(rs[:], s_ps[s][:, 0:1]))
                        tstep.settle()
                        nc.vector.scalar_tensor_tensor(o[:], acc_ps[s][:], rs[:], gbias[:], ALU.mult, ALU.add).then_inc(eo_step, 1)
                        dve.wait_ge(eo_step, t + 1)
                        nc.vector.tensor_scalar(eo[:], o[:], 0.0, None, ALU.min).then_inc(eo_in, 1)
                        dve.wait_ge(y_done, t + 3)
                        tstep.done(nc.vector.scalar_tensor_tensor(res[:], o[:], 0.0, y_ps[s][:], ALU.max, ALU.add))
                        dve.wait_ge(eo_ready, t + 1)
                        tstep.settle()
                        dve.wait_ge(x2_out[s], 16 * i + 16)
                        tstep.done(nc.vector.scalar_tensor_tensor(x2[s][:], eo[:], -1.0, res[:], ALU.add, ALU.add))
                        tstep.settle()
                        dve.sem_inc(x2_ready, 1)

                    for t, s, i, last_tile in tiles_behind(dve):
                        first, limit, shift = visit_range(dve, t)
                        inverses(t)
                        dve.wait_ge(acc_done, t + 1)
                        nc.vector.tensor_scalar(diag[s][:], C["ident"], w_self[:, ds(t, 1)], None, ALU.mult).then_inc(diag_ready, 1)
                        nc.vector.tensor_scalar(window[:], C["iota_row"], C["tile_start"][:, ds(t, 1)], None, ALU.add)
                        hold(dve, tile_in[s], 64 * i + 64)
                        if last_tile:
                            dve.wait_ge(total_ready, t)
                        nc.vector.memset(w_sum, 0.0).then_inc(sum_zeroed, 1)
                        hold(dve, sum_zeroed, t + 1)
                        with dve.Fori(first, limit, VT) as at_tile:
                            v = dve.snap(((at_tile + shift) & 0xFFFF) >> (VT.bit_length() - 1))
                            for half in (0, 1):
                                slots = range(half * HT, half * HT + HT)
                                dve.wait_ge(w_ready, 2 * v + half + 1)
                                for j in slots:
                                    last = nc.vector.tensor_scalar(cap[:, j, :], window[:], dst_col[:, ds(at_tile + j, 1)], -1e30, ALU.not_equal, ALU.mult)
                                last.then_inc(argp_ready, 1)
                                dve.wait_ge(argq_ready, 2 * v + half + 1)
                                for j in slots:
                                    last = nc.vector.scalar_tensor_tensor(argp[:, j, :], pqb[s][:, 0, :], es_col[:, ds(at_tile + j, 1)],
                                                                          argq[:, j, :], ALU.add, ALU.max)
                                last.then_inc(argp_ready, 1)
                                dve.wait_ge(argp_ready, 4 * v + 2 * half + 2)
                                hs = slice(half * HT, half * HT + HT)
                                nc.vector.tensor_tensor(argp[:, hs, :], argp[:, hs, :], cap[:, hs, :], ALU.min).then_inc(arg_ready, 1)
                            for half in (0, 1):
                                dve.wait_ge(w_ready, 2 * v + half + 3)
                                dve.wait_ge(summed, 2 * v + half + 2)
                                nc.vector.tensor_reduce(W[:, 1 - half, 0, :], W[:, half].rearrange("p j n -> p n j"), AX.X, ALU.add).then_inc(summed, 1)
                            hold(dve, summed, 2 * v + 4)
                        nc.vector.tensor_copy(w_total[s][:], w_sum).then_inc(total_ready, 1)
                        queries(t, s)
                        if last_tile:
                            finish(*last_tile)
                    finish(NT - 1, 0, NT // 2)

        graph.close()

        with ExitStack() as ex:
            w1 = sb(ex, "w1", [P, NE, KC, F])
            w2 = sb(ex, "w2", [P, NE, FC, D])
            b1 = sb(ex, "b1", [1, NE, F])
            b2 = sb(ex, "b2", [P, NE, D])
            gamma = sb(ex, "gamma", [P, NE, D])
            beta = sb(ex, "beta", [P, NE, D])
            router = sb(ex, "router", [P, KC, NE])
            logits = sb(ex, "logits", [P, NT, NE])
            gates = sb(ex, "gates", [P, 2, NT])
            slot_of = sb(ex, "slot_of", [P, 2, NT], I32)
            token_of = sb(ex, "token_of", [P, P], I32)
            expert_of = sb(ex, "expert_of", [1, ST], I32)
            weights_in = sem("expert_weights_in")

            XR = 4
            with ExitStack() as no:
                xb = [sb(no, f"fxb{s}", [P, D]) for s in range(XR)]
                xf, xfT = ([sb(no, f"{n}{s}", [P, D]) for s in (0, 1)] for n in ("fxf", "fxfT"))
                bn, mv, sd = ([sb(no, f"{n}{s}", [P, w]) for s in (0, 1)] for n, w in (("fbn", 6), ("fmv", 2), ("fsd", 2)))
                T_ps, l_ps = ([psum(no, f"{n}{s}") for s in (0, 1)] for n in ("fT_ps", "fl_ps"))
                x_in, xf_out = [sem(f"fx_in{s}") for s in range(XR)], [sem(f"fxf_out{s}") for s in (0, 1)]
                (router_in, bn_ready, mv_ready, rstd_ready, xf_ready, T_done, xfT_ready, l_done, l_ready) = (
                    sem("f_" + n) for n in ("router_in", "bn_ready", "mv_ready", "rstd_ready", "xf_ready", "T_done",
                                            "xfT_ready", "l_done", "l_ready"))
                with nc.Block() as block:
                    @block.sync
                    def _(sp):
                        sp.dma_start(router[:], a["router"]).then_inc(router_in, 16)
                        for t, s, i in tiles(sp, NT, XR):
                            sp.wait_ge(xf_ready, t + 1)
                            sp.dma_start(xb[s][:], x2_rows[ds(t * P, P), :]).then_inc(x_in[s], 16)

                    @block.gpsimd
                    def _(pool):
                        for dst, src in ((w1[:], a["w1"]), (w2[:], a["w2"]), (b1[:], a["b1"]), (b2[:], a["b2"].partition_broadcast(P)),
                                         (gamma[:], a["gamma"].partition_broadcast(P)), (beta[:], a["beta"].partition_broadcast(P))):
                            nc.gpsimd.dma_start(dst, src).then_inc(weights_in, 16)
                        for t, s, i in tiles(pool):
                            pool.wait_ge(mv_ready, t + 1)
                            nc.gpsimd.tensor_tensor(sd[s][:, 0:1], mv[s][:, 1:2], C["ln_eps"], ALU.add).then_inc(rstd_ready, 1)
                            pool.wait_ge(rstd_ready, 2 * t + 1)
                            nc.gpsimd.tensor_tensor(sd[s][:, 1:2], sd[s][:, 0:1], C["minus_half"], ALU.pow).then_inc(rstd_ready, 1)

                    @block.vector
                    def _(dve):
                        dve.sem_inc(xf_ready, XR)

                        def moments(t, x, i):
                            s = x % 2
                            dve.wait_ge(x_in[x], 16 * i + 16)
                            nc.vector.bn_stats(bn[s][:], xb[x][:]).then_inc(bn_ready, 1)
                            hold(dve, bn_ready, t + 1)
                            nc.vector.bn_aggr(mv[s][:], bn[s][:]).then_inc(mv_ready, 1)

                        moments(0, 0, 0)
                        for t, x, i in tiles(dve, NT, XR):
                            s = x % 2
                            if not isinstance(t, int):
                                moments(t + 1, (x + 1) % XR, i + (x + 1) // XR)
                            dve.wait_ge(mv_ready, t + 1)
                            dve.wait_ge(rstd_ready, 2 * t + 2)
                            dve.wait_ge(xf_out[s], 16 * (XR // 2 * i + x // 2) + 16)
                            dve.wait_ge(T_done, t + 1)
                            nc.vector.tensor_scalar(xf[s][:], xb[x][:], mv[s][:, 0:1], sd[s][:, 1:2], ALU.subtract, ALU.mult).then_inc(xf_ready, 1)

                    @block.scalar
                    def _(act):
                        for s in (0, 1):
                            act.sem_inc(xf_out[s], 16)
                        act.sem_inc(l_ready, 2)

                        def turn(t, s):
                            act.wait_ge(xf_ready, t + 1 + XR)
                            act.dma_start(xf_rows[ds(t * P, P), :], xf[s][:]).then_inc(xf_out[s], 16)
                            act.wait_ge(T_done, t + 3)
                            act.wait_ge(l_ready, t + 1)
                            nc.scalar.copy(xfT[s][:], T_ps[s][:]).then_inc(xfT_ready, 1)

                        turn(0, 0)
                        for t, s, i in tiles(act):
                            if not isinstance(t, int):
                                turn(t + 1, 1 - s)
                            hold(act, l_done, t + 1)
                            nc.scalar.copy(logits[:, ds(t, 1), :], l_ps[s][:, 0:NE].unsqueeze(1)).then_inc(l_ready, 1)
                        act.wait_ge(xf_out[0], 16 * (NT // 2 + 2))
                        act.wait_ge(xf_out[1], 16 * (NT // 2 + 1))

                    @block.tensor
                    def _(pe):
                        pe.wait_ge(router_in, 16)
                        pe.sem_inc(T_done, 2)
                        pe.sem_inc(xfT_ready, 2)

                        def turn(t, s):
                            pe.wait_ge(xf_ready, t + 1 + XR)
                            pe.wait_ge(xfT_ready, t + 1)
                            for c in range(KC):
                                last = nc.tensor.transpose(T_ps[s][:, c * P:(c + 1) * P], xf[s][:, c * P:(c + 1) * P], C["ident"])
                            last.then_inc(T_done, 1)

                        turn(0, 0)
                        for t, s, i in tiles(pe):
                            if not isinstance(t, int):
                                turn(t + 1, 1 - s)
                            pe.wait_ge(xfT_ready, t + 3)
                            pe.wait_ge(l_ready, t + 1)
                            for c in range(KC):
                                last = nc.tensor.matmul(l_ps[s][:, 0:NE], xfT[s][:, c * P:(c + 1) * P], router[:, c, :], start=(c == 0), stop=(c == KC - 1))
                            last.then_inc(l_done, 1)

            with ExitStack() as ro:
                top, first, dif = sb(ro, "top_logit", [P, 2, NT]), sb(ro, "first", [P, NT]), sb(ro, "dif", [P, 2, NT])
                rest, spare = sb(ro, "rest", [P, NT, NE]), sb(ro, "spare", [P, NT, NE])
                pick = sb(ro, "pick", [P, 2, NT, NE])
                picked_by = sb(ro, "picked_by", [P, NT, NE])
                run = [sb(ro, f"run{s}", [P, NT, NE]) for s in (0, 1)]
                end = [sb(ro, f"end{s}", [P, NE]) for s in (0, 1)]
                filled, filled_i = sb(ro, "filled", [P, NE]), sb(ro, "filled_i", [P, NE], I32)
                start = sb(ro, "start_of", [P, NE])
                slot_f, listed_i, part_i = sb(ro, "slot_f", [P, 2, NT]), sb(ro, "listed_i", [P, 2, NT], I32), sb(ro, "part_i", [P, 2, NT], I32)
                hi, lo = sb(ro, "slot_hi", [P, 2, NT]), sb(ro, "slot_lo", [P, 2, NT])
                at_or_past, owner = sb(ro, "at_or_past", [1, ST, NE]), sb(ro, "owner", [1, ST])
                hot_hi, hot_lo = ([sb(ro, f"{n}{k}", [P, P]) for k in (0, 1)] for n in ("hot_hi", "hot_lo"))
                zero16 = sb(ro, "zero16", [P, P], BF16)
                ahead_ps, count_ps, token_ps = psum(ro, "ahead_ps"), psum(ro, "count_ps"), psum(ro, "token_ps")
                r_step, dif_ready, exp_ready, picks_ready, picks_counted, hot_ready, hot_used, zero_ready, tokens_done = (
                    sem("r_" + n) for n in ("step", "dif_ready", "exp_ready", "picks_ready", "picks_counted", "hot_ready", "hot_used",
                                            "zero_ready", "tokens_done"))
                with nc.Block() as block:
                    @block.gpsimd
                    def _(pool):
                        nc.gpsimd.memset(zero16[:], 0.0).then_inc(zero_ready, 1)

                    @block.scalar
                    def _(act):
                        act.wait_ge(dif_ready, 1)
                        nc.scalar.activation(dif[:, 1, :], dif[:, 0, :], ACT.Exp).then_inc(exp_ready, 1)

                    @block.tensor
                    def _(pe):
                        flat = lambda v: v.rearrange("p t e -> p (t e)")
                        pe.wait_ge(picks_ready, 1)
                        nc.tensor.matmul(ahead_ps[:, 0:NT * NE], C["before"], flat(picked_by[:]), start=True, stop=True)
                        nc.tensor.matmul(count_ps[:, 0:NT * NE], C["ones_row"], flat(picked_by[:]), start=True, stop=True).then_inc(picks_counted, 1)
                        pe.wait_ge(zero_ready, 1)
                        nc.tensor.matmul(token_ps[:, 0:P], zero16[:], zero16[:], start=True, stop=False, skip_group_check=True)
                        with pe.Fori(0, NT) as t:
                            for k in (0, 1):
                                pe.wait_ge(hot_ready, 2 * t + k + 1)
                                nc.tensor.matmul(token_ps[:, 0:P], hot_lo[k][:], hot_hi[k][:], start=False, stop=False, skip_group_check=True).then_inc(hot_used, 1)
                        nc.tensor.matmul(token_ps[:, 0:P], zero16[:], zero16[:], start=False, stop=True, skip_group_check=True).then_inc(tokens_done, 1)

                    @block.vector
                    def _(dve):
                        steps = Steps(dve, r_step, 0)
                        dve.sem_inc(hot_used, 2)

                        def step(ins):
                            steps.done(ins)
                            steps.settle()

                        every_expert = lambda v: v.unsqueeze(2).broadcast_to([P, NT, NE])
                        every_tile = lambda v: v.unsqueeze(1).broadcast_to([P, NT, NE])
                        V = nc.vector
                        expert_id = every_tile(C["iota_row"][:, 0:NE])
                        for k, left in ((0, logits), (1, rest)):
                            step(V.tensor_reduce(top[:, k, :], left[:], AX.X, ALU.max))
                            step(V.tensor_tensor(spare[:], left[:], every_expert(top[:, k, :]), ALU.is_equal))
                            step(V.scalar_tensor_tensor(spare[:], spare[:], -100.0, expert_id, ALU.mult, ALU.add))
                            step(V.tensor_reduce(first[:], spare[:], AX.X, ALU.min))
                            step(V.tensor_scalar(first[:], first[:], 100.0, None, ALU.add))
                            step(V.tensor_tensor(pick[:, k], expert_id, every_expert(first[:]), ALU.is_equal))
                            if k == 0:
                                step(V.scalar_tensor_tensor(rest[:], pick[:, 0], -3e38, logits[:], ALU.mult, ALU.add))
                        V.tensor_tensor(dif[:, 0, :], top[:, 1, :], top[:, 0, :], ALU.subtract).then_inc(dif_ready, 1)
                        for k in (0, 1):
                            step(V.tensor_tensor(pick[:, k], pick[:, k], every_expert(C["real"]), ALU.mult))
                        V.tensor_tensor(picked_by[:], pick[:, 0], pick[:, 1], ALU.add).then_inc(picks_ready, 1)
                        dve.wait_ge(exp_ready, 1)
                        step(V.tensor_scalar(first[:], dif[:, 1, :], 1.0, None, ALU.add))
                        step(V.reciprocal(gates[:, 0, :], first[:]))
                        step(V.tensor_tensor(gates[:, 1, :], dif[:, 1, :], gates[:, 0, :], ALU.mult))
                        dve.wait_ge(picks_counted, 1)
                        step(V.tensor_copy(run[0][:], count_ps[:, 0:NT * NE].rearrange("p (t e) -> p t e", e=NE)))
                        side, width = 0, 1
                        while width < NT:
                            V.tensor_copy(run[1 - side][:, 0:width, :], run[side][:, 0:width, :])
                            step(V.tensor_tensor(run[1 - side][:, width:, :], run[side][:, width:, :], run[side][:, 0:NT - width, :], ALU.add))
                            side, width = 1 - side, 2 * width
                        upto, other = run[side], run[1 - side]
                        step(V.tensor_scalar(filled[:], upto[:, NT - 1, :], float(P - 1), None, ALU.add))
                        step(V.tensor_copy(filled_i[:], filled[:]))
                        step(V.tensor_scalar(filled_i[:], filled_i[:], P.bit_length() - 1, None, ALU.arith_shift_right))
                        V.tensor_copy(end[0][:], filled_i[:])
                        step(V.tensor_copy(filled[:], filled_i[:]))
                        eside, width = 0, 1
                        while width < NE:
                            V.tensor_copy(end[1 - eside][:, 0:width], end[eside][:, 0:width])
                            step(V.tensor_tensor(end[1 - eside][:, width:], end[eside][:, width:], end[eside][:, 0:NE - width], ALU.add))
                            eside, width = 1 - eside, 2 * width
                        ends = end[eside]
                        step(V.tensor_tensor(start[:], ends[:], filled[:], ALU.subtract))
                        step(V.tensor_tensor(other[:], upto[:], count_ps[:, 0:NT * NE].rearrange("p (t e) -> p t e", e=NE), ALU.subtract))
                        step(V.tensor_tensor(other[:], other[:], ahead_ps[:, 0:NT * NE].rearrange("p (t e) -> p t e", e=NE), ALU.add))
                        step(V.scalar_tensor_tensor(other[:], every_tile(start[:]), float(P), other[:], ALU.mult, ALU.add))
                        for k in (0, 1):
                            step(V.tensor_tensor(spare[:], pick[:, k], other[:], ALU.mult))
                            step(V.tensor_reduce(slot_f[:, k, :], spare[:], AX.X, ALU.add))
                        step(V.tensor_copy(slot_of[:], slot_f[:]))
                        step(V.tensor_tensor(slot_f[:], slot_f[:], C["past_end"].unsqueeze(1).broadcast_to([P, 2, NT]), ALU.add))
                        step(V.tensor_copy(listed_i[:], slot_f[:]))
                        step(V.tensor_scalar(part_i[:], listed_i[:], P.bit_length() - 1, None, ALU.arith_shift_right))
                        step(V.tensor_copy(hi[:], part_i[:]))
                        step(V.tensor_scalar(part_i[:], listed_i[:], P - 1, None, ALU.bitwise_and))
                        step(V.tensor_copy(lo[:], part_i[:]))
                        step(V.tensor_tensor(at_or_past[:], C["iota_row"][0:1, 0:ST].unsqueeze(2).broadcast_to([1, ST, NE]),
                                             ends[0:1, :].unsqueeze(1).broadcast_to([1, ST, NE]), ALU.is_ge))
                        step(V.tensor_reduce(owner[:], at_or_past[:], AX.X, ALU.add))
                        step(V.tensor_scalar(owner[:], owner[:], float(NE - 1), None, ALU.min))
                        step(V.tensor_copy(expert_of[:], owner[:]))
                        with dve.Fori(0, NT) as t:
                            for k in (0, 1):
                                dve.wait_ge(hot_used, 2 * t + k + 1)
                                V.tensor_scalar(hot_hi[k][:], C["iota_row"], hi[:, k, ds(t, 1)], None, ALU.is_equal)
                                V.tensor_scalar(hot_lo[k][:], C["iota_row"], lo[:, k, ds(t, 1)], C["node_id"][:, ds(t, 1)],
                                                ALU.is_equal, ALU.mult).then_inc(hot_ready, 1)
                        dve.wait_ge(tokens_done, 1)
                        step(V.tensor_copy(token_of[:], token_ps[:, 0:P]))

            with ExitStack() as ep:
                two = lambda name, shape, dt=F32: [sb(ep, f"{name}{s}", shape, dt) for s in (0, 1)]
                rows, rowsT, hid, hidT = two("xs", [P, D]), two("xsT", [P, D]), two("hid", [P, F]), two("hidT", [P, F])
                z0, z, zn, zg, y = two("z0", [P, D]), two("z", [P, D]), two("zn", [P, D]), two("zg", [P, D]), two("y", [P, D])
                idx2, zbn, zmv, zsd = two("idx2", [P, 1], I32), two("zbn", [P, 6]), two("zmv", [P, 2]), two("zsd", [P, 2])
                T_ps, hT_ps = psum(ep, "xT_ps"), psum(ep, "hT_ps")
                hid_ps, o_ps = ([psum(ep, f"{n}{s}") for s in (0, 1)] for n in ("hid_ps", "o_ps"))
                rows_in, y_out = ([sem(f"{n}{s}") for s in (0, 1)] for n in ("xs_in", "y_out"))
                (idx_copied, T_done, T_ready, hid_done, hid_ready, hT_done, hT_ready, o_done, z0_ready, z_ready, zbn_ready, zmv_ready,
                 zvar_ready, zsd_ready, zn_ready, y_ready) = (sem("e_" + n) for n in (
                     "idx_copied", "T_done", "T_ready", "hid_done", "hid_ready", "hT_done", "hT_ready", "o_done", "z0_ready", "z_ready",
                     "zbn_ready", "zmv_ready", "zvar_ready", "zsd_ready", "zn_ready", "y_ready"))

                def expert(eng, t):
                    return eng.value_load(expert_of[:, ds(t, 1)], min_val=0, max_val=NE - 1)

                with nc.Block() as block:
                    @block.sync
                    def _(sp):
                        for s in (0, 1):
                            sp.sem_inc(y_out[s], 16)
                        for t, s, i in tiles(sp, ST):
                            sp.wait_ge(y_ready, t + 1)
                            sp.dma_start(y_rows[ds(t * P, P), :], y[s][:]).then_inc(y_out[s], 16)
                        sp.wait_ge(y_out[0], 16 * (ST // 2 + 2))
                        sp.wait_ge(y_out[1], 16 * (ST // 2 + 1))

                    @block.gpsimd
                    def _(pool):
                        pool.wait_ge(weights_in, 16 * 6)

                        def gather(t, s):
                            hold(pool, T_done, t + 1)
                            hold(pool, z0_ready, t + 1)
                            nc.gpsimd.tensor_copy(idx2[s][:], token_of[:, ds(t, 1)]).then_inc(idx_copied, 1)
                            hold(pool, idx_copied, t + 1)
                            nc.gpsimd.indirect_dma_start(rows[s][:], None, xf_rows, bass.IndirectOffsetOnAxis(ap=idx2[s][:, 0:1], axis=0)).then_inc(rows_in[s], 16)

                        def base(t, s, i):
                            e = expert(pool, t)
                            pool.wait_ge(rows_in[s], 16 * i + 16)
                            pool.wait_ge(z_ready, t + 1)
                            nc.gpsimd.tensor_tensor(z0[s][:], rows[s][:], b2[:, ds(e, 1), :].rearrange("p o d -> p (o d)"), ALU.add).then_inc(z0_ready, 1)

                        pool.sem_inc(z0_ready, 2)
                        gather(0, 0)
                        gather(1, 1)
                        base(0, 0, 0)
                        gather(2, 0)
                        for t, s, i in tiles(pool, ST):
                            if not isinstance(t, int):
                                base(t + 1, 1 - s, i + s)
                                gather(t + 3, 1 - s)
                            pool.wait_ge(zmv_ready, t + 1)
                            nc.gpsimd.tensor_tensor(zsd[s][:, 0:1], zmv[s][:, 1:2], C["ffn_eps"], ALU.add).then_inc(zvar_ready, 1)
                            pool.wait_ge(zvar_ready, t + 1)
                            nc.gpsimd.tensor_tensor(zsd[s][:, 1:2], zsd[s][:, 0:1], C["minus_half"], ALU.pow).then_inc(zsd_ready, 1)
                        pool.wait_ge(rows_in[0], 16 * (ST // 2 + 2))
                        pool.wait_ge(rows_in[1], 16 * (ST // 2 + 1))

                    @block.scalar
                    def _(act):
                        def turned(t, s):
                            act.wait_ge(T_done, t + 3)
                            act.wait_ge(hid_done, t + 1)
                            nc.scalar.copy(rowsT[s][:], T_ps[:]).then_inc(T_ready, 1)

                        def relu(t, s):
                            act.wait_ge(hid_done, t + 3)
                            act.wait_ge(hT_done, t + 1)
                            nc.scalar.activation(hid[s][:], hid_ps[s][:, 0:F], ACT.Relu).then_inc(hid_ready, 1)

                        turned(0, 0)
                        turned(1, 1)
                        relu(0, 0)
                        for t, s, i in tiles(act, ST):
                            act.wait_ge(hT_done, t + 3)
                            act.wait_ge(o_done, t + 1)
                            nc.scalar.copy(hidT[s][:], hT_ps[:, 0:F]).then_inc(hT_ready, 1)
                            if not isinstance(t, int):
                                relu(t + 1, 1 - s)
                                turned(t + 2, s)

                    @block.tensor
                    def _(pe):
                        pe.wait_ge(weights_in, 16 * 6)
                        for one in (T_done, hid_done, hT_done, o_done):
                            pe.sem_inc(one, 2)

                        def turn(t, s, i):
                            pe.wait_ge(rows_in[s], 16 * i + 16)
                            for c in range(KC):
                                last = nc.tensor.transpose(T_ps[:, c * P:(c + 1) * P], rows[s][:, c * P:(c + 1) * P], C["ident"])
                            last.then_inc(T_done, 1)

                        def hidden(t, s):
                            e = expert(pe, t)
                            pe.wait_ge(T_ready, t + 1)
                            for c in range(KC):
                                nc.tensor.matmul(hid_ps[s][:, 0:F], rowsT[s][:, c * P:(c + 1) * P], w1[:, ds(e, 1), c, :].rearrange("p o f -> p (o f)"),
                                                 start=(c == 0), stop=False)
                            nc.tensor.matmul(hid_ps[s][:, 0:F], C["ones_row"][0:1, :], b1[:, ds(e, 1), :].rearrange("p o f -> p (o f)"),
                                             start=False, stop=True).then_inc(hid_done, 1)

                        turn(0, 0, 0)
                        pe.wait_ge(T_ready, 1)
                        turn(1, 1, 0)
                        hidden(0, 0)
                        for t, s, i in tiles(pe, ST):
                            pe.wait_ge(hid_ready, t + 1)
                            for f in range(FC):
                                last = nc.tensor.transpose(hT_ps[:, f * P:(f + 1) * P], hid[s][:, f * P:(f + 1) * P], C["ident"])
                            last.then_inc(hT_done, 1)
                            if not isinstance(t, int):
                                hidden(t + 1, 1 - s)
                            e = expert(pe, t)
                            pe.wait_ge(hT_ready, t + 1)
                            pe.wait_ge(z_ready, t + 1)
                            for f in range(FC):
                                last = nc.tensor.matmul(o_ps[s][:], hidT[s][:, f * P:(f + 1) * P], w2[:, ds(e, 1), f, :].rearrange("p o d -> p (o d)"),
                                                        start=(f == 0), stop=(f == FC - 1))
                            last.then_inc(o_done, 1)
                            if not isinstance(t, int):
                                turn(t + 2, s, i + 1)

                    @block.vector
                    def _(dve):
                        dve.wait_ge(weights_in, 16 * 6)
                        dve.sem_inc(z_ready, 2)
                        def scale(t, s, i):
                            e = expert(dve, t)
                            dve.wait_ge(zmv_ready, t + 1)
                            dve.wait_ge(zsd_ready, t + 1)
                            nc.vector.tensor_scalar(zn[s][:], z[s][:], zmv[s][:, 0:1], zsd[s][:, 1:2], ALU.subtract, ALU.mult).then_inc(zn_ready, 1)
                            dve.wait_ge(zn_ready, 2 * t + 1)
                            nc.vector.tensor_tensor(zg[s][:], zn[s][:], gamma[:, ds(e, 1), :].rearrange("p o d -> p (o d)"), ALU.mult).then_inc(zn_ready, 1)
                            dve.wait_ge(zn_ready, 2 * t + 2)
                            dve.wait_ge(y_out[s], 16 * i + 16)
                            nc.vector.tensor_tensor(y[s][:], zg[s][:], beta[:, ds(e, 1), :].rearrange("p o d -> p (o d)"), ALU.add).then_inc(y_ready, 1)

                        for t, s, i, last_tile in tiles_behind(dve, ST):
                            dve.wait_ge(o_done, t + 3)
                            dve.wait_ge(z0_ready, t + 3)
                            nc.vector.tensor_tensor(z[s][:], o_ps[s][:], z0[s][:], ALU.add).then_inc(z_ready, 1)
                            hold(dve, z_ready, t + 3)
                            nc.vector.bn_stats(zbn[s][:], z[s][:]).then_inc(zbn_ready, 1)
                            hold(dve, zbn_ready, t + 1)
                            nc.vector.bn_aggr(zmv[s][:], zbn[s][:]).then_inc(zmv_ready, 1)
                            if last_tile:
                                scale(*last_tile)
                        scale(ST - 1, 0, ST // 2)

            with ExitStack() as co:
                xb, ya, yb, part, ob = ([sb(co, f"{n}{s}", [P, D]) for s in (0, 1)] for n in ("cx", "ya", "yb", "part", "ob"))
                idx3 = [sb(co, f"idx3{s}", [P, 2], I32) for s in (0, 1)]
                x_in, o_out = ([sem(f"{n}{s}") for s in (0, 1)] for n in ("cx_in", "co_out"))
                y_in = [[sem(f"y_in{s}{k}") for k in (0, 1)] for s in (0, 1)]
                idx_copied, part_ready, out_ready = sem("c_idx_copied"), sem("c_part_ready"), sem("c_out_ready")
                with nc.Block() as block:
                    @block.sync
                    def _(sp):
                        for t, s, i in tiles(sp):
                            sp.wait_ge(out_ready, t + 1)
                            sp.dma_start(xb[s][:], x2_rows[ds(t * P, P), :]).then_inc(x_in[s], 16)

                    @block.gpsimd
                    def _(pool):
                        for t, s, i in tiles(pool):
                            hold(pool, out_ready, t + 1)
                            nc.gpsimd.tensor_copy(idx3[s][:], slot_of[:, :, ds(t, 1)].rearrange("p k o -> p (k o)")).then_inc(idx_copied, 1)
                            hold(pool, idx_copied, t + 1)
                            for k, rows in ((0, ya), (1, yb)):
                                nc.gpsimd.indirect_dma_start(rows[s][:], None, y_rows, bass.IndirectOffsetOnAxis(ap=idx3[s][:, k:k + 1], axis=0)).then_inc(y_in[s][k], 16)

                    @block.vector
                    def _(dve):
                        dve.sem_inc(out_ready, 2)
                        for t, s, i in tiles(dve):
                            dve.wait_ge(x_in[s], 16 * i + 16)
                            dve.wait_ge(y_in[s][0], 16 * i + 16)
                            nc.vector.scalar_tensor_tensor(part[s][:], ya[s][:], gates[:, 0, ds(t, 1)], xb[s][:], ALU.mult, ALU.add).then_inc(part_ready, 1)
                            dve.wait_ge(part_ready, t + 1)
                            dve.wait_ge(y_in[s][1], 16 * i + 16)
                            dve.wait_ge(o_out[s], 16 * i + 16)
                            nc.vector.scalar_tensor_tensor(ob[s][:], yb[s][:], gates[:, 1, ds(t, 1)], part[s][:], ALU.mult, ALU.add).then_inc(out_ready, 1)

                    @block.scalar
                    def _(act):
                        for s in (0, 1):
                            act.sem_inc(o_out[s], 16)
                        for t, s, i in tiles(act):
                            act.wait_ge(out_ready, t + 3)
                            act.dma_start(out[ds(t * P, P), :], ob[s][:]).then_inc(o_out[s], 16)
                        act.wait_ge(o_out[0], 16 * (NT // 2 + 2))
                        act.wait_ge(o_out[1], 16 * (NT // 2 + 1))


def lay_out(inputs):
    f = lambda n: np.asarray(inputs[n])
    pad = lambda v, n, c: np.concatenate([v, np.full((n - v.shape[0],) + v.shape[1:], c, v.dtype)])
    rows = lambda w: np.ascontiguousarray(w.reshape(-1, P, w.shape[-1]).transpose(1, 0, 2))
    src, dst = pad(f("src"), EP, 0), pad(f("dst"), EP, NO_NODE)
    temp = f("L0_mix_temperature").reshape(KC, 2)
    return {
        "consts": const_layout()[0],
        "x": pad(f("x"), NP, 0),
        "src_col": np.ascontiguousarray(src.reshape(ET, P).T), "dst_col": np.ascontiguousarray(dst.reshape(ET, P).T),
        "src_lin": src.reshape(ROWP, -1), "dst_lin": dst.reshape(ROWP, -1), 
        "wg": rows(f("L0_gnn_W").T), "w_nat": rows(f("L0_gnn_W")),
        "avec": rows(np.stack([f("L0_gnn_a_src"), f("L0_gnn_a_dst")], 1)),
        "gbias": f("L0_gnn_bias"), "pbias": f("L0_mix_bproj"),
        "wqkv": rows(f("L0_mix_Wqkv").T), "wproj": rows(f("L0_mix_Wproj").T),
        "temp": np.ascontiguousarray(np.repeat(temp, 64, axis=1).T),
        "router": rows(f("L0_ffn_router_w")),
        "w1": np.ascontiguousarray(f("L0_ffn_w1").reshape(NE, KC, P, F).transpose(2, 0, 1, 3)),
        "w2": np.ascontiguousarray(f("L0_ffn_w2").reshape(NE, FC, P, D).transpose(2, 0, 1, 3)),
        "b1": f("L0_ffn_b1")[None],
        "b2": f("L0_ffn_b2"), "gamma": f("L0_ffn_gamma"), "beta": f("L0_ffn_beta"),
    }


def kernel(**inputs):
    import concourse.bacc as _bacc
    from concourse.bass_utils import run_bass_kernel_spmd as _run

    nc = _bacc.Bacc("TRN2", target_bir_lowering=False, num_devices=1)
    arrays = {f"in_{n}": v for n, v in lay_out(inputs).items()}
    a = {n[3:]: nc.dram_tensor(n, v.shape, mybir.dt.from_np(v.dtype), kind="ExternalInput").ap() for n, v in arrays.items()}
    out = nc.dram_tensor("out", (NP, D), F32, kind="ExternalOutput").ap()
    gps_layer(nc, a, out)
    return _run(nc, [arrays], core_ids=[0]).results[0]["out"][:N]
```
